# Optimizing a Trainium2 kernel written in Bass

```python
import numpy as np
import jax
import jax.numpy as jnp

def _softmax(x, axis=-1):
    return jax.nn.softmax(x, axis=axis)

def _gelu(x):
    return jax.nn.gelu(x, approximate=True)

def _silu(x):
    return jax.nn.silu(x)

def _sigmoid(x):
    return jax.nn.sigmoid(x)

def _layernorm(x, axis=-1, eps=1e-05):
    m = jnp.mean(x, axis=axis, keepdims=True)
    v = jnp.var(x, axis=axis, keepdims=True)
    return (x - m) / jnp.sqrt(v + eps)

def _scatter_add(tgt, idx, src, axis=0):
    return tgt.at[idx].add(src)

def _segment_sum(src, seg, n):
    return jax.ops.segment_sum(src, seg, n)
kernel_name = 'mk_conv_attn_hybrid_d2_conv_nchw128_r2_6cfd5d'

def setup_inputs(seed: int=0):
    np.random.seed(seed)
    _w = jnp.asarray

    def _rec_inputs():
        import jax
        import jax.numpy as jnp
        _gk = jax.random.key(seed)
        x = -0.000929 + 1 * jax.random.normal(jax.random.fold_in(_gk, 1), (2, 64, 32, 32), jnp.float32)
        return x
    x = _rec_inputs()

    def _L0_conv_setup():
        import jax, jax.numpy as jnp
        import numpy as np
        B, C, H, W = (2, 64, 32, 32)
        NUM_HEADS = 8
        GN_GROUPS = 8
        GN_EPS = 1e-05
        key = jax.random.key(seed)
        ks = jax.random.split(key, 11)
        s = 0.02
        return {'x': jax.random.normal(ks[0], (B, C, H, W), dtype=jnp.float32), 'Wq': jax.random.normal(ks[1], (C, C), dtype=jnp.float32) * s, 'bq': jnp.zeros((C,), dtype=jnp.float32), 'Wk': jax.random.normal(ks[2], (C, C), dtype=jnp.float32) * s, 'bk': jnp.zeros((C,), dtype=jnp.float32), 'Wv': jax.random.normal(ks[3], (C, C), dtype=jnp.float32) * s, 'bv': jnp.zeros((C,), dtype=jnp.float32), 'Wo': jax.random.normal(ks[4], (C, C), dtype=jnp.float32) * s, 'bo': jnp.zeros((C,), dtype=jnp.float32), 'gn_w': jnp.ones((C,), dtype=jnp.float32), 'gn_b': jnp.zeros((C,), dtype=jnp.float32)}
    _L0_conv_all = _L0_conv_setup()
    _L0_conv_in = {k: v for k, v in _L0_conv_all.items() if k in ('Wq', 'bq', 'Wk', 'bk', 'Wv', 'bv', 'Wo', 'bo', 'gn_w', 'gn_b')}
    del _L0_conv_all

    def _L1_attn_setup():
        import jax, jax.numpy as jnp
        import numpy as np
        B, N, D = (8, 1024, 64)
        N_LAYER, N_HEAD = (4, 8)
        PARAMS_STD = 0.05

        def _attention(V, Q, Z):
            n = Z.shape[1]
            Attn = jnp.einsum('bni,ij,bmj->bnm', Z, Q, Z)
            values = jnp.einsum('ij,bnj->bni', V, Z)
            return jnp.einsum('bnm,bmi->bni', Attn, values) / n
        key = jax.random.key(seed)
        kz, kv, kq = jax.random.split(key, 3)
        Z = jax.random.normal(kz, (B, N, D), dtype=jnp.float32)
        v_matrix = PARAMS_STD * jax.random.normal(kv, (N_LAYER, N_HEAD, 1, D, D), dtype=jnp.float32)
        q_matrix = PARAMS_STD * jax.random.normal(kq, (N_LAYER, N_HEAD, 1, D, D), dtype=jnp.float32)
        return {'Z': Z, 'v_matrix': v_matrix, 'q_matrix': q_matrix}
    _L1_attn_all = _L1_attn_setup()
    _L1_attn_in = {k: v for k, v in _L1_attn_all.items() if k in ('v_matrix', 'q_matrix')}
    del _L1_attn_all

    def _L1_ffn_setup():
        import jax, jax.numpy as jnp
        import numpy as np
        B, N, D, C, E, K = (8, 4096, 64, 64, 8, 2)
        key = jax.random.key(seed)
        k0, k1, k2 = jax.random.split(key, 3)
        x = jax.random.normal(k0, (B, N, D), dtype=jnp.float32)
        router_w = jax.random.normal(k1, (D, E), dtype=jnp.float32) * 0.05
        router_b = jnp.zeros((E,), dtype=jnp.float32)
        expert_w = jax.random.normal(k2, (E, D, C), dtype=jnp.float32) * (1.0 / np.sqrt(D))
        expert_b = jnp.zeros((E, C), dtype=jnp.float32)
        return {'x': x, 'router_w': router_w, 'router_b': router_b, 'expert_w': expert_w, 'expert_b': expert_b}
    _L1_ffn_all = _L1_ffn_setup()
    _L1_ffn_in = {k: v for k, v in _L1_ffn_all.items() if k in ('router_w', 'router_b', 'expert_w', 'expert_b')}
    del _L1_ffn_all
    return {'x': x, 'L0_conv_Wq': _L0_conv_in['Wq'], 'L0_conv_bq': _L0_conv_in['bq'], 'L0_conv_Wk': _L0_conv_in['Wk'], 'L0_conv_bk': _L0_conv_in['bk'], 'L0_conv_Wv': _L0_conv_in['Wv'], 'L0_conv_bv': _L0_conv_in['bv'], 'L0_conv_Wo': _L0_conv_in['Wo'], 'L0_conv_bo': _L0_conv_in['bo'], 'L0_conv_gn_w': _L0_conv_in['gn_w'], 'L0_conv_gn_b': _L0_conv_in['gn_b'], 'L1_attn_v_matrix': _L1_attn_in['v_matrix'], 'L1_attn_q_matrix': _L1_attn_in['q_matrix'], 'L1_ffn_router_w': _L1_ffn_in['router_w'], 'L1_ffn_router_b': _L1_ffn_in['router_b'], 'L1_ffn_expert_w': _L1_ffn_in['expert_w'], 'L1_ffn_expert_b': _L1_ffn_in['expert_b']}

def reference(x, L0_conv_Wq, L0_conv_bq, L0_conv_Wk, L0_conv_bk, L0_conv_Wv, L0_conv_bv, L0_conv_Wo, L0_conv_bo, L0_conv_gn_w, L0_conv_gn_b, L1_attn_v_matrix, L1_attn_q_matrix, L1_ffn_router_w, L1_ffn_router_b, L1_ffn_expert_w, L1_ffn_expert_b):
    import jax
    import jax.numpy as jnp

    def _L0_conv_ref(x, Wq, bq, Wk, bk, Wv, bv, Wo, bo, gn_w, gn_b):
        import jax, jax.numpy as jnp
        import numpy as np
        B, C, H, W = (2, 64, 32, 32)
        NUM_HEADS = 8
        GN_GROUPS = 8
        GN_EPS = 1e-05
        b, c, h, w = x.shape
        nh = NUM_HEADS
        dh = c // nh
        scale = dh ** (-0.5)
        x_seq = x.reshape(b, c, h * w).transpose(0, 2, 1)

        def proj(W, bias):
            y = jnp.einsum('bnc,dc->bnd', x_seq, W) + bias
            return y.reshape(b, -1, nh, dh).transpose(0, 2, 1, 3)
        q = proj(Wq, bq)
        k = proj(Wk, bk)
        v = proj(Wv, bv)
        attn = jnp.einsum('bhnd,bhmd->bhnm', q, k) * scale
        attn = jax.nn.softmax(attn, axis=-1)
        out = jnp.einsum('bhnm,bhmd->bhnd', attn, v)
        out = out.transpose(0, 2, 1, 3).reshape(b, -1, c)
        out = jnp.einsum('bnc,dc->bnd', out, Wo) + bo
        out = out.transpose(0, 2, 1).reshape(b, c, h, w)
        g = GN_GROUPS
        og = out.reshape(b, g, c // g, h, w)
        mean = jnp.mean(og, axis=(2, 3, 4), keepdims=True)
        var = jnp.var(og, axis=(2, 3, 4), keepdims=True)
        og = (og - mean) * jax.lax.rsqrt(var + GN_EPS)
        normed = og.reshape(b, c, h, w) * gn_w[None, :, None, None] + gn_b[None, :, None, None]
        return normed + x

    def _L1_attn_ref(Z, v_matrix, q_matrix):
        import jax, jax.numpy as jnp
        import numpy as np
        B, N, D = (8, 1024, 64)
        N_LAYER, N_HEAD = (4, 8)
        PARAMS_STD = 0.05

        def _attention(V, Q, Z):
            n = Z.shape[1]
            Attn = jnp.einsum('bni,ij,bmj->bnm', Z, Q, Z)
            values = jnp.einsum('ij,bnj->bni', V, Z)
            return jnp.einsum('bnm,bmi->bni', Attn, values) / n
        n_layer, n_head = (v_matrix.shape[0], v_matrix.shape[1])
        for i in range(n_layer):
            Zi = Z
            residues = jnp.zeros_like(Zi)
            for j in range(n_head):
                Vij = v_matrix[i, j, 0]
                Qij = q_matrix[i, j, 0]
                residues = residues + _attention(Vij, Qij, Zi)
            Z = Zi + residues / n_head
        return Z

    def _L1_ffn_ref(x, router_w, router_b, expert_w, expert_b):
        import jax, jax.numpy as jnp
        import numpy as np
        B, N, D, C, E, K = (8, 4096, 64, 64, 8, 2)
        router_probs = jax.nn.softmax(x @ router_w + router_b, axis=-1)
        top_p, top_i = jax.lax.top_k(router_probs, K)
        top_p = top_p / jnp.sum(top_p, axis=-1, keepdims=True)
        expert_out = jnp.einsum('bnd,edc->bnec', x, expert_w) + expert_b
        gathered = jnp.take_along_axis(expert_out, top_i[..., None], axis=2)
        return jnp.einsum('bnk,bnkc->bnc', top_p, gathered)

    def _gn(v, G=32, eps=1e-05):
        B_, C_, H_, W_ = v.shape
        g = v.reshape(B_, G, C_ // G, H_, W_)
        m = jnp.mean(g, axis=(2, 3, 4), keepdims=True)
        s = jnp.var(g, axis=(2, 3, 4), keepdims=True)
        return ((g - m) / jnp.sqrt(s + eps)).reshape(v.shape)

    def _ln_c(v, eps=1e-06):
        m = jnp.mean(v, axis=1, keepdims=True)
        s = jnp.var(v, axis=1, keepdims=True)
        return (v - m) / jnp.sqrt(s + eps)

    def _ln_t(v, eps=1e-05):
        m = jnp.mean(v, axis=-1, keepdims=True)
        s = jnp.var(v, axis=-1, keepdims=True)
        return (v - m) / jnp.sqrt(s + eps)

    def _to_tokens(v):
        B_, C_, H_, W_ = v.shape
        return v.reshape(B_, C_, H_ * W_).transpose(0, 2, 1)

    def _from_tokens(t, like):
        B_, C_, H_, W_ = like.shape
        return t.transpose(0, 2, 1).reshape(B_, C_, H_, W_)
    x = _L0_conv_ref(x, L0_conv_Wq, L0_conv_bq, L0_conv_Wk, L0_conv_bk, L0_conv_Wv, L0_conv_bv, L0_conv_Wo, L0_conv_bo, L0_conv_gn_w, L0_conv_gn_b)
    t = _to_tokens(x)
    t = t + _L1_attn_ref(_ln_t(t), L1_attn_v_matrix, L1_attn_q_matrix)
    t = t + _L1_ffn_ref(_ln_t(t), L1_ffn_router_w, L1_ffn_router_b, L1_ffn_expert_w, L1_ffn_expert_b)
    x = _from_tokens(t, x)
    return x

_drawn_inputs = setup_inputs


def setup_inputs(seed=0):
    import zlib

    import numpy as np

    out = dict(_drawn_inputs(seed))
    spreads = {'L0_conv_bq': (0.0, 0.8),
     'L0_conv_bk': (0.0, 0.8),
     'L0_conv_bv': (0.0, 0.1),
     'L0_conv_bo': (0.0, 0.1),
     'L0_conv_gn_w': (1.0, 0.2),
     'L0_conv_gn_b': (0.0, 0.1),
     'L1_ffn_router_b': (0.0, 0.1),
     'L1_ffn_expert_b': (0.0, 0.317)}
    factors = {'L0_conv_Wq': 6.742, 'L0_conv_Wk': 8.0, 'L0_conv_Wv': 4.363}
    for name, (base, spread) in spreads.items():
        noise = np.random.default_rng([zlib.crc32(name.encode()), seed]).standard_normal(out[name].shape)
        drawn = base * np.exp(spread * noise) if base else spread * noise
        out[name] = jnp.asarray(drawn.astype(out[name].dtype))
    for name, factor in factors.items():
        out[name] = (out[name] * factor).astype(out[name].dtype)
    return out
```

```python
from contextlib import ExitStack

import concourse.bass as bass
from concourse import mybir

ALU = mybir.AluOpType
ACT = mybir.ActivationFunctionType
AX_X = mybir.AxisListType.X
F32 = mybir.dt.float32
BF16 = mybir.dt.bfloat16
U32 = mybir.dt.uint32

P = 128
B = 2
C = 64
N = 1024
H = 8
DH = C // H
HG = 4
NG = H // HG
NH = 512
HALVES = N // NH
TT = N // P
QT = NH // P
BLOCKS = [(b, g, hf) for b in range(B) for g in range(NG) for hf in range(HALVES)]
UNITS = TT * len(BLOCKS)
VW = 32
LAYERS = 4
NHEAD = 8
E = 8
SCALE = float(DH) ** -0.5
EPS = 1e-5

PARTS = 3
STORED = PARTS + 2
PART_ROWS = DH * PARTS
ZERO_FROM = 64
MAX_ROW = 96
SCORE_ROWS = MAX_ROW + 3

LEAD = 13
PV_LAG = 2
ST_BANKS = (4, 5, 6)
PV_BANK = 7
P_RING = 4
IN_REST = 10
YT_BANKS = (6, 7, 0, 1)
GB_BANKS = (3, 4, 5, 0)
MOE_BANKS = (6, 7)
GB_LAG = 3
MOE = [(c, b, k) for c in range(2) for b in range(B) for k in range(E // 2)]


def conv_attn_hybrid_kernel(nc, x, wqk, wv, wo, cols, bv_row, vt, qt, router, expw, expb, rb_row, consts, cbf, ones, out):
    with ExitStack() as ctx:
        def sb(name, shape, dt=F32):
            return ctx.enter_context(nc.sbuf_tensor(name, shape, dt))

        def sem(name):
            return ctx.enter_context(nc.semaphore(name))

        parts_dram = nc.dram_tensor("parts_scratch", (B, STORED, P, N), BF16, kind="Internal").ap()
        max_dram = nc.dram_tensor("max_scratch", (len(BLOCKS), 3 * HG * QT, P), BF16, kind="Internal").ap()
        psum = ctx.enter_context(nc.psum_tensor("psum", [P, 8, 512], F32))

        cen2 = psum[:, 2:6, :].rearrange("p a (h n) -> p (a h) n", h=2)

        x_sb = sb("x_sb", [P, N])
        wqk_sb = sb("wqk_sb", [P, B, P])
        wv_sb = sb("wv_sb", [P, P])
        wo_sb = sb("wo_sb", [P, P])
        cols_sb = sb("cols_sb", [P, 4])
        bv_sb = sb("bv_sb", [P, P])
        vt_sb = sb("vt_sb", [P, LAYERS, NHEAD * C])
        qt_sb = sb("qt_sb", [P, LAYERS * NHEAD, P])
        rw_sb = sb("rw_sb", [P, B * E])
        expw_sb = sb("expw_sb", [P, E // 2, C])
        expb_sb = sb("expb_sb", [P, P])
        rb_sb = sb("rb_sb", [P, E])
        consts_sb = sb("consts_sb", [P, 6, P])
        ident, centre, neg_avg, avg, diag_mask, ident_n = (consts_sb[:, i, :] for i in range(6))
        weight_sb = sb("weight_sb", [P, E])
        cbf_sb = sb("cbf_sb", [P, 1 + B * E // 2, P], BF16)
        ident_bf = cbf_sb[:, 0, :]
        select = cbf_sb[:, 1:, :]

        part = [sb(f"part{i}", [P, B, N], BF16) for i in range(3)]
        rest = sb("rest", [P, B, N])
        qop = sb("qop", [P, B, H, N], BF16)
        kop = sb("kop", [P, B, H, N], BF16)
        v_aug = sb("v_aug", [P, TT, B, H, VW])
        negmax = sb("negmax", [P, 2, HG * QT])
        max_rest = sb("max_rest", [P, 2, HG * QT])
        max_part = sb("max_part", [P, 2, 3, HG * QT], BF16)
        max_row = sb("max_row", [3 * HG * QT, 2, P], BF16)
        probs = sb("probs", [P, P_RING, HG, NH])
        o_sb = sb("o_sb", [P, 2, NH])
        rden = sb("rden", [P, 2, QT, HG])
        attn = sb("attn", [P, TT, B, C])

        spare_q = qop[:].rearrange("p b h n -> p (b h n)").bitcast(F32)
        y = spare_q[:, 0:2 * N].rearrange("p (t b u c) -> p t b u c", t=TT, b=B, u=2)
        yt2 = spare_q[:, 2 * N:4 * N].rearrange("p (b n) -> p b n", b=B)
        scaled = spare_q[:, 4 * N:6 * N].rearrange("p (i n) -> p i n", n=NH)
        res = spare_q[:, 6 * N:7 * N]
        spare = probs[:].rearrange("p u j n -> p (u j n)").rearrange("p (a n) -> p a n", n=N)
        attn_t, proj, aff, t1, z_t, t2 = (spare[:, i, :] for i in range(6))
        z, sq = (spare[:, i, :].rearrange("p (t c) -> p t c", c=P) for i in (6, 7))
        bn = sb("bn", [P, 2, 6])
        mv = sb("mv", [P, 2])
        neg_mean, diff, dev, grstd, gain, shift = (sb(n, [P, 1]) for n in ("neg_mean", "diff", "dev", "grstd", "gain", "shift"))
        ssq = sb("ssq", [P, TT * B])
        rstd = sb("rstd", [P, TT * B])
        var_eps = sb("var_eps", [P, TT * B])
        gvar_eps = sb("gvar_eps", [P, 1])
        minus_half = sb("minus_half", [P, TT * B])
        gram = sb("gram", [P, P])
        gv = sb("gv", [P, NHEAD, C])
        w_l = sb("w_l", [P, P])
        u_l = sb("u_l", [P, P])
        tt_l = sb("tt_l", [P, P])
        tt_f = sb("tt_f", [P, P])
        cen_rw = sb("cen_rw", [P, P + B * E])
        lg = sb("lg", [P, TT * B, E])
        lg2 = sb("lg2", [P, TT * B, E])
        m1 = sb("m1", [P, TT * B])
        m2 = sb("m2", [P, TT * B])
        cand = sb("cand", [P, TT * B, E])
        pick = sb("pick", [P, TT * B])
        hot1 = sb("hot1", [P, TT * B, E])
        hot2 = sb("hot2", [P, TT * B, E])
        dlt = sb("dlt", [P, TT * B])
        ed = sb("ed", [P, TT * B])
        gate1 = sb("gate1", [P, TT * B])
        gate2 = sb("gate2", [P, TT * B])
        gates = sb("gates", [P, TT * B, E])
        gate_rest = sb("gate_rest", [P, TT * B, E])
        gate_part = sb("gate_part", [P, TT, P], BF16)
        gate_t = sb("gate_t", [P, N], BF16)
        expb_part = sb("expb_part", [P, 3, P], BF16)
        expb_rest = sb("expb_rest", [P, P])

        names = (
            "in_x in_qk in_c in_v in_rest zeroed_q zeroed_q1 zeroed_k zeroed_v v_ready qk_full part_h part_r part_m part_l v_full "
            "slot_full slot_free st_full exp_done pv_done o_copied out_written pool_chain max_split max_out "
            "dve_chain at_full at_sb0 at_sb1 wo_full proj_ready crw_full crw_ready mean_ready mean_full dev_ready var_full "
            "aff_ready affine_done t1_ready cen1_full sq1_ready z_ready gram0_full zt_full zt_ready gv_full gv_act gv_dve "
            "m_full w_ready u_full u_ready tt_full tt_ready gram_full gram_ready attn2_full t2_ready cen2_full sq2_ready "
            "y_ready yt_full yt_ready logits_read delta_ready exp2_ready gates_ready gate_zeroed gate_split gt_full "
            "gt_ready vareps_ready rstd_ready gb_full scaled_ready moe_done out_done expb_split").split()
        S = {n: sem(n) for n in names}
        ops_ready = [[sem(f"ops_ready{b}{g}") for g in range(NG)] for b in range(B)]
        mrow_in = [sem(f"mrow_in{i}") for i in range(2)]
        N_OPS = 2 * PARTS
        parts_out = [sem(f"parts_out{b}") for b in range(B)]

        jobs_at = {}
        for u in range(-LEAD, UNITS + 8):
            v = u + LEAD
            jobs = []
            if 0 <= v < UNITS:
                blk, k = divmod(v, TT)
                jobs += [("max", blk, (2 * k) // QT, (2 * k) % QT), ("max", blk, (2 * k + 1) // QT, (2 * k + 1) % QT)]
            if v >= TT + 1 and (v - 1) % TT == 0 and (v - 1) // TT <= len(BLOCKS):
                jobs.append(("max_t", (v - 1) // TT - 1, 0, 0))
            w = u - PV_LAG - 1
            if w >= TT and w % TT == 0 and w // TT <= len(BLOCKS):
                jobs.append(("out_t", w // TT - 1, 0, 0))
            jobs_at[u] = jobs
        SLOT_JOBS = [j for u in range(-LEAD, UNITS + 8) for j in jobs_at[u]]

        def jobs_until(kind, blk):
            return max(r for r, job in enumerate(SLOT_JOBS) if job[:2] == (kind, blk)) + 1

        block = ctx.enter_context(nc.Block())

        @block.sync
        def _(sp):
            sp.dma_start(x_sb[:], x).then_inc(S["in_x"], 16)
            sp.dma_start(cols_sb[:], cols).then_inc(S["in_qk"], 16)
            sp.dma_start(wqk_sb[:], wqk).then_inc(S["in_qk"], 16)
            sp.dma_start(wv_sb[:], wv).then_inc(S["in_v"], 16)
            sp.dma_start(bv_sb[:], bv_row).then_inc(S["in_v"], 16)
            sp.dma_start(cbf_sb[:], cbf.rearrange("p (a n) -> p a n", n=P)).then_inc(S["in_c"], 16)
            sp.dma_start(kop[MAX_ROW:SCORE_ROWS, :, :, :], ones).then_inc(S["in_c"], 16)
            sp.wait_ge(S["zeroed_q"], 1)
            sp.wait_ge(S["zeroed_k"], 1)
            for b in range(B):
                for i, name in enumerate(("part_h", "part_m", "part_l")):
                    sp.wait_ge(S[name], HALVES * (b + 1))
                    for stored in range(i, STORED, PARTS):
                        sp.dma_start(parts_dram[b, stored, :, :], part[i][:, b, :]).then_inc(parts_out[b], 16)
                sp.wait_ge(parts_out[b], 16 * STORED)
                if b == 1:
                    sp.wait_ge(S["zeroed_q1"], 1)
                    sp.wait_ge(S["zeroed_k"], 2)
                rows = parts_dram[b].rearrange("s (d w h) n -> (s d) w (h n)", d=DH, w=2)
                for g in range(NG):
                    at_g = slice(g * HG * N, (g + 1) * HG * N)
                    for r in range(PARTS):
                        to = slice(r * PART_ROWS, (r + 1) * PART_ROWS)
                        sp.dma_start(qop[to, b, g * HG:(g + 1) * HG, :],
                                     rows[0:PART_ROWS, 0, at_g]).then_inc(ops_ready[b][g], 16)
                        sp.dma_start(kop[to, b, g * HG:(g + 1) * HG, :],
                                     rows[r * DH:r * DH + PART_ROWS, 1, at_g]).then_inc(ops_ready[b][g], 16)
                if b == 0:
                    sp.dma_start(consts_sb[:], consts[:, 0:6 * P].rearrange("p (a n) -> p a n", n=P)).then_inc(S["in_rest"], 16)
                    sp.dma_start(weight_sb[:], consts[:, 6 * P:6 * P + E]).then_inc(S["in_rest"], 16)
                    sp.dma_start(cen_rw[:, 0:P], consts[:, P:2 * P]).then_inc(S["in_rest"], 16)
                    sp.dma_start(rw_sb[:], router).then_inc(S["in_rest"], 16)
                    sp.dma_start(wo_sb[:], wo).then_inc(S["in_rest"], 16)
                    sp.dma_start(expw_sb[:], expw).then_inc(S["in_rest"], 16)
                    sp.dma_start(expb_sb[:], expb).then_inc(S["in_rest"], 16)
                    sp.dma_start(rb_sb[:], rb_row).then_inc(S["in_rest"], 16)
                    sp.dma_start(vt_sb[:], vt).then_inc(S["in_rest"], 16)
                    sp.dma_start(qt_sb[:], qt).then_inc(S["in_rest"], 16)
            for i, (b, g, hf) in enumerate(BLOCKS):
                sp.wait_ge(S["slot_free"], jobs_until("max_t", i))
                sp.dma_start(max_dram[i], max_row[:, i % 2, :]).then_inc(S["max_out"], 16)
                sp.wait_ge(S["max_out"], 16 * (i + 1))
                sp.dma_start(qop[MAX_ROW:SCORE_ROWS, b, g * HG:(g + 1) * HG, hf * NH:(hf + 1) * NH],
                             max_dram[i].rearrange("(s j t) n -> s j (t n)", s=PARTS, j=HG)).then_inc(mrow_in[i % 2], 16)
            for c in range(2):
                sp.wait_ge(S["out_done"], c + 1)
                sp.dma_start(out[:, c * NH:(c + 1) * NH], res[:, c * NH:(c + 1) * NH]).then_inc(S["out_written"], 16)
            sp.wait_ge(S["out_written"], 32)

        @block.tensor
        def _(pe):
            pe.wait_ge(S["in_x"], 16)
            pe.wait_ge(S["in_qk"], 32)
            for i in range(B * HALVES):
                b, hf = divmod(i, HALVES)
                nc.tensor.matmul(psum[:, 4 + i, :], wqk_sb[:, b, :], x_sb[:, hf * NH:(hf + 1) * NH],
                                 start=True, stop=True).then_inc(S["qk_full"], 1)
            pe.wait_ge(S["in_v"], 32)
            for t in range(TT):
                last = nc.tensor.matmul(psum[:, 2 + t // 4, (t % 4) * P:(t % 4 + 1) * P], x_sb[:, t * P:(t + 1) * P],
                                        wv_sb[:], start=True, stop=True, skip_group_check=True)
            last.then_inc(S["v_full"], 1)

            slot = [0]

            def fill_slot(job):
                kind, blk, j, t = job
                r = slot[0]
                slot[0] += 1
                if r >= 2:
                    pe.wait_ge(S["slot_free"], r - 1)
                b, g, hf = BLOCKS[blk]
                if kind == "max":
                    if j == 0 and t == 0:
                        pe.wait_ge(ops_ready[b][g], 16 * N_OPS)
                    if r == 1:
                        pe.wait_ge(S["v_ready"], 1)
                    q = qop[0:MAX_ROW, b, g * HG + j, hf * NH + t * P:hf * NH + (t + 1) * P]
                    for c in range(2):
                        last = nc.tensor.matmul(psum[:, 2 * (r % 2) + c, :], q,
                                                kop[0:MAX_ROW, b, g * HG + j, c * NH:(c + 1) * NH], start=True, stop=True)
                elif kind == "max_t":
                    pe.wait_ge(S["max_split"], blk + 1)
                    pe.wait_ge(S["in_c"], 32)
                    dst = psum[0:3 * HG * QT, 2 * (r % 2), 0:P // 2].bitcast(BF16)
                    last = nc.tensor.transpose(dst, max_part[:, blk % 2, :, :], ident_bf)
                else:
                    pe.wait_ge(S["o_copied"], blk + 1)
                    pe.wait_ge(S["in_rest"], 16 * IN_REST)
                    for q in range(QT):
                        last = nc.tensor.transpose(psum[:, 2 * (r % 2), q * P:(q + 1) * P],
                                                   o_sb[:, blk % 2, q * P:(q + 1) * P], ident)
                last.then_inc(S["slot_full"], 1)

            def scores(u, j):
                blk, mt = divmod(u, TT)
                b, g, hf = BLOCKS[blk]
                s = HG * u + j
                if mt == 0 and j == 0:
                    pe.wait_ge(mrow_in[blk % 2], 16 * (blk // 2 + 1))
                if s >= len(ST_BANKS):
                    pe.wait_ge(S["exp_done"], s - len(ST_BANKS) + 1)
                elif s == 0:
                    pe.wait_ge(S["in_c"], 32)
                    pe.wait_ge(S["part_r"], B * HALVES)
                nc.tensor.matmul(psum[:, ST_BANKS[s % len(ST_BANKS)], :],
                                 kop[0:SCORE_ROWS, b, g * HG + j, mt * P:(mt + 1) * P],
                                 qop[0:SCORE_ROWS, b, g * HG + j, hf * NH:(hf + 1) * NH],
                                 start=True, stop=True).then_inc(S["st_full"], 1)

            def values(u):
                blk, mt = divmod(u, TT)
                b, g, hf = BLOCKS[blk]
                pe.wait_ge(S["exp_done"], HG * (u + 1))
                if mt == 0 and blk:
                    pe.wait_ge(S["o_copied"], blk)
                if u == 0:
                    pe.wait_ge(S["v_ready"], 1)
                for j in range(HG):
                    last = nc.tensor.matmul(psum[j * VW:(j + 1) * VW, PV_BANK, :], v_aug[:, mt, b, g * HG + j, :],
                                            probs[:, u % P_RING, j, :], start=mt == 0, stop=mt == TT - 1,
                                            skip_group_check=True)
                last.then_inc(S["pv_done"], 1)

            for u in range(-LEAD, UNITS + 8):
                jobs = list(jobs_at[u])
                for j in range(HG):
                    if 0 <= u < UNITS:
                        scores(u, j)
                    if j % 2 and jobs:
                        fill_slot(jobs.pop(0))
                while jobs:
                    fill_slot(jobs.pop(0))
                if 0 <= u - PV_LAG < UNITS:
                    values(u - PV_LAG)

            pe.wait_ge(S["slot_free"], len(SLOT_JOBS))
            for t in range(TT):
                last = nc.tensor.transpose(psum[:, t // 4, (t % 4) * P:(t % 4 + 1) * P], attn[:, t, :, :], ident)
                if t % 4 == 3:
                    last.then_inc(S["at_full"], 1)
            nc.tensor.matmul(psum[:, 6, 0:B * E], centre, rw_sb[:], start=True, stop=True).then_inc(S["crw_full"], 1)
            for c in range(2):
                pe.wait_ge(S[f"at_sb{c}"], 1)
                nc.tensor.matmul(psum[:, 2 + c, :], wo_sb[:], attn_t[:, c * NH:(c + 1) * NH],
                                 start=True, stop=True).then_inc(S["wo_full"], 1)
            pe.wait_ge(S["mean_ready"], 1)
            nc.tensor.matmul(psum[:, 4, 0:1], neg_avg, mv[:, 0:1], start=True, stop=True).then_inc(S["mean_full"], 1)
            pe.wait_ge(S["dev_ready"], 1)
            nc.tensor.matmul(psum[:, 5, 0:1], avg, dev[:], start=True, stop=True).then_inc(S["var_full"], 1)
            for c in range(2):
                pe.wait_ge(S["t1_ready"], c + 1)
                for t in range(4 * c, 4 * c + 4):
                    last = nc.tensor.matmul(psum[:, c, (t % 4) * P:(t % 4 + 1) * P], t1[:, t * P:(t + 1) * P], centre,
                                            start=True, stop=True, skip_group_check=True)
                last.then_inc(S["cen1_full"], 1)
            for c in range(2):
                pe.wait_ge(S["z_ready"], c + 1)
                for t in range(4 * c, 4 * c + 4):
                    last = nc.tensor.matmul(psum[:, 6, 0:P], z[:, t, :], z[:, t, :], start=t == 0, stop=t == TT - 1)
            last.then_inc(S["gram0_full"], 1)
            for c in range(2):
                for t in range(4 * c, 4 * c + 4):
                    last = nc.tensor.transpose(psum[:, 2 + c, (t % 4) * P:(t % 4 + 1) * P], z[:, t, :], ident)
                last.then_inc(S["zt_full"], 1)
            for l in range(LAYERS):
                pe.wait_ge(S["gram_ready"], l + 1)
                if l:
                    pe.wait_ge(S["tt_ready"], l)
                for c in range(2):
                    nc.tensor.matmul(psum[:, (7, 5)[c], 0:NHEAD * C // 2], gram[:],
                                     vt_sb[:, l, c * NHEAD * C // 2:(c + 1) * NHEAD * C // 2],
                                     start=True, stop=True).then_inc(S["gv_full"], 1)
                nc.tensor.matmul(psum[:, 4, 0:P], ident_n, ident, start=True, stop=False)
                for j in range(NHEAD):
                    if j == 0:
                        pe.wait_ge(S["gv_act"], l + 1)
                    if j == NHEAD // 2:
                        pe.wait_ge(S["gv_dve"], l + 1)
                    last = nc.tensor.matmul(psum[:, 4, 0:P], qt_sb[:, l * NHEAD + j, :],
                                            gv[:, j:j + 1, :].broadcast_to([P, B, C]), start=False, stop=j == NHEAD - 1)
                last.then_inc(S["m_full"], 1)
                pe.wait_ge(S["w_ready"], l + 1)
                if l < LAYERS - 1:
                    nc.tensor.matmul(psum[:, 6, 0:P], gram[:], w_l[:], start=True, stop=True).then_inc(S["u_full"], 1)
                    nc.tensor.matmul(psum[:, 7, 0:P], w_l[:], tt_l[:] if l else ident,
                                     start=True, stop=True).then_inc(S["tt_full"], 1)
                    pe.wait_ge(S["u_ready"], l + 1)
                    nc.tensor.matmul(psum[:, 5, 0:P], w_l[:], u_l[:], start=True, stop=True).then_inc(S["gram_full"], 1)
                else:
                    nc.tensor.matmul(psum[:, 7, 0:P], tt_l[:], w_l[:], start=True, stop=True).then_inc(S["tt_full"], 1)
            pe.wait_ge(S["tt_ready"], LAYERS)
            pe.wait_ge(S["zt_ready"], 2)
            for c in range(2):
                nc.tensor.matmul(psum[:, c, :], tt_f[:], z_t[:, c * NH:(c + 1) * NH],
                                 start=True, stop=True).then_inc(S["attn2_full"], 1)
            pe.wait_ge(S["crw_ready"], 1)
            for c in range(2):
                pe.wait_ge(S["t2_ready"], c + 1)
                for t in range(4 * c, 4 * c + 4):
                    last = nc.tensor.matmul(cen2[:, t, 0:P + B * E], t2[:, t * P:(t + 1) * P], cen_rw[:],
                                            start=True, stop=True, skip_group_check=True)
                last.then_inc(S["cen2_full"], 1)
            for c in range(2):
                pe.wait_ge(S["y_ready"], c + 1)
                for b in range(B):
                    for t in range(4 * c, 4 * c + 4):
                        last = nc.tensor.transpose(psum[:, YT_BANKS[2 * c + b], (t % 4) * P:(t % 4 + 1) * P],
                                                   y[:, t, b, :, :], ident)
                    last.then_inc(S["yt_full"], 1)
            pe.wait_ge(S["gate_split"], 1)
            pe.wait_ge(S["logits_read"], 1)
            for t in range(TT):
                last = nc.tensor.transpose(psum[:, 2, t * P // 2:(t + 1) * P // 2].bitcast(BF16), gate_part[:, t, :],
                                           ident_bf)
            last.then_inc(S["gt_full"], 1)
            pe.wait_ge(S["gt_ready"], 1)
            pe.wait_ge(S["expb_split"], 1)
            pe.wait_ge(S["yt_ready"], 4)
            for c in range(2):
                for s in range(3):
                    nc.tensor.matmul(psum[:, MOE_BANKS[c], :], expb_part[:, s, :], gate_t[:, c * NH:(c + 1) * NH],
                                     start=s == 0, stop=False, skip_group_check=True)
            for i in range(len(MOE) + GB_LAG):
                if i < len(MOE):
                    c, b, k = MOE[i]
                    if i >= len(GB_BANKS):
                        pe.wait_ge(S["scaled_ready"], i - len(GB_BANKS) + 1)
                    nc.tensor.matmul(psum[:, GB_BANKS[i % len(GB_BANKS)], :], select[:, b * (E // 2) + k, :],
                                     gate_t[:, c * NH:(c + 1) * NH], start=True, stop=True).then_inc(S["gb_full"], 1)
                if i >= GB_LAG:
                    c, b, k = MOE[i - GB_LAG]
                    pe.wait_ge(S["scaled_ready"], i - GB_LAG + 1)
                    nc.tensor.matmul(psum[b * C:(b + 1) * C, MOE_BANKS[c], :], expw_sb[:, k, :],
                                     scaled[:, (i - GB_LAG) % 4, :], start=False, stop=k == E // 2 - 1,
                                     skip_group_check=True).then_inc(S["moe_done"], 1)

        @block.gpsimd
        def _(pool):
            def zero(op, b):
                return nc.gpsimd.memset(op[ZERO_FROM:MAX_ROW, b, :, :].bitcast(U32), 0)

            zero(kop, 0).then_inc(S["zeroed_k"], 1)
            pool.wait_ge(S["zeroed_k"], 1)
            nc.gpsimd.memset(v_aug[:], 0.0).then_inc(S["pool_chain"], 1)
            pool.wait_ge(S["pool_chain"], 1)
            nc.gpsimd.memset(v_aug[:, :, :, :, DH:DH + 1], 1.0).then_inc(S["zeroed_v"], 1)
            pool.wait_ge(S["zeroed_v"], 1)
            zero(kop, 1).then_inc(S["zeroed_k"], 1)
            pool.wait_ge(S["zeroed_k"], 2)
            zero(qop, 1).then_inc(S["zeroed_q1"], 1)
            pool.wait_ge(S["zeroed_q1"], 1)
            nc.gpsimd.memset(minus_half[:], -0.5).then_inc(S["pool_chain"], 1)
            pool.wait_ge(S["pool_chain"], 2)
            chain = [2]

            def link(ins):
                chain[0] += 1
                ins.then_inc(S["pool_chain"], 1)
                pool.wait_ge(S["pool_chain"], chain[0])

            split_done = {}

            def split(first, parts, rest_, last_inc):
                link(nc.gpsimd.tensor_copy(parts[0], first))
                link(nc.gpsimd.tensor_tensor(rest_, first, parts[0], ALU.subtract))
                link(nc.gpsimd.tensor_copy(parts[1], rest_))
                nc.gpsimd.tensor_tensor(parts[2], rest_, parts[1], ALU.subtract).then_inc(S[last_inc], 1)
                split_done[last_inc] = split_done.get(last_inc, 0) + 1
                pool.wait_ge(S[last_inc], split_done[last_inc])

            for blk in range(len(BLOCKS)):
                pool.wait_ge(S["slot_free"], jobs_until("max", blk))
                if blk >= 2:
                    pool.wait_ge(S["slot_free"], jobs_until("max_t", blk - 2))
                i = blk % 2
                split(negmax[:, i, :], [max_part[:, i, s, :] for s in range(3)], max_rest[:, i, :], "max_split")
                if blk == 0:
                    nc.gpsimd.memset(gate_part[:].bitcast(U32), 0).then_inc(S["gate_zeroed"], 1)
                    pool.wait_ge(S["gate_zeroed"], 1)
                    pool.wait_ge(S["in_rest"], 16 * IN_REST)
                    split(expb_sb[:], [expb_part[:, s, :] for s in range(3)], expb_rest[:], "expb_split")

            for i in range(5):
                pool.wait_ge(S["vareps_ready"], i + 1)
                r = slice(8 * ((i - 1) % 2), 8 * ((i - 1) % 2) + 8)
                if i == 0:
                    ins = nc.gpsimd.tensor_tensor(grstd[:], gvar_eps[:], minus_half[:, 0:1], ALU.pow)
                else:
                    ins = nc.gpsimd.tensor_tensor(rstd[:, r], var_eps[:, r], minus_half[:, r], ALU.pow)
                ins.then_inc(S["rstd_ready"], 1)
                pool.wait_ge(S["rstd_ready"], i + 1)

        @block.scalar
        def _(act):
            act.wait_ge(S["in_qk"], 32)
            for i in range(B * HALVES):
                b, hf = divmod(i, HALVES)
                cols_i = slice(hf * NH, (hf + 1) * NH)
                act.wait_ge(S["qk_full"], i + 1)
                nc.scalar.activation(part[0][:, b, cols_i], psum[:, 4 + i, :], ACT.Identity,
                                     bias=cols_sb[:, 0:1]).then_inc(S["part_h"], 1)
                act.wait_ge(S["part_r"], i + 1)
                nc.scalar.activation(part[1][:, b, cols_i], rest[:, b, cols_i], ACT.Copy).then_inc(S["part_m"], 1)
            for u in range(UNITS + PV_LAG + 1):
                if u < UNITS:
                    if u >= P_RING:
                        act.wait_ge(S["pv_done"], u - P_RING + 1)
                    for j in range(HG):
                        s = HG * u + j
                        act.wait_ge(S["st_full"], s + 1)
                        nc.scalar.activation(probs[:, u % P_RING, j, :], psum[:, ST_BANKS[s % len(ST_BANKS)], :],
                                             ACT.Exp, scale=SCALE).then_inc(S["exp_done"], 1)
                w = u - PV_LAG - (TT - 1)
                if w >= 0 and w % TT == 0:
                    blk = w // TT
                    act.wait_ge(S["pv_done"], TT * (blk + 1))
                    if blk >= 2:
                        act.wait_ge(S["slot_free"], jobs_until("out_t", blk - 2))
                    nc.scalar.activation(o_sb[:, blk % 2, :], psum[:, PV_BANK, :], ACT.Copy).then_inc(S["o_copied"], 1)

            act.wait_ge(S["at_full"], 1)
            nc.scalar.activation(attn_t[:, 0:NH], psum[:, 0, :], ACT.Copy).then_inc(S["at_sb0"], 1)
            act.wait_ge(S["crw_full"], 1)
            nc.scalar.activation(cen_rw[:, P:], psum[:, 6, 0:B * E], ACT.Copy).then_inc(S["crw_ready"], 1)
            for c in range(2):
                act.wait_ge(S["wo_full"], c + 1)
                nc.scalar.activation(proj[:, c * NH:(c + 1) * NH], psum[:, 2 + c, :], ACT.Identity,
                                     bias=cols_sb[:, 1:2]).then_inc(S["proj_ready"], 1)
            act.wait_ge(S["aff_ready"], 1)
            for c in range(2):
                nc.scalar.activation(aff[:, c * NH:(c + 1) * NH], proj[:, c * NH:(c + 1) * NH], ACT.Identity,
                                     bias=shift[:], scale=gain[:]).then_inc(S["affine_done"], 1)
            for c in range(2):
                act.wait_ge(S["cen1_full"], c + 1)
                nc.scalar.activation(sq[:, 4 * c:4 * c + 4, :], psum[:, c, :].rearrange("p (t c) -> p t c", t=4),
                                     ACT.Square).then_inc(S["sq1_ready"], 1)
            for c in range(2):
                act.wait_ge(S["zt_full"], c + 1)
                nc.scalar.activation(z_t[:, c * NH:(c + 1) * NH], psum[:, 2 + c, :], ACT.Copy).then_inc(S["zt_ready"], 1)
            for l in range(LAYERS):
                act.wait_ge(S["gv_full"], 2 * l + 1)
                nc.scalar.activation(gv[:, 0:NHEAD // 2, :],
                                     psum[:, 7, 0:NHEAD * C // 2].rearrange("p (j c) -> p j c", c=C),
                                     ACT.Copy).then_inc(S["gv_act"], 1)
                act.wait_ge(S["tt_full"], l + 1)
                nc.scalar.activation(tt_l[:] if l < LAYERS - 1 else tt_f[:], psum[:, 7, 0:P],
                                     ACT.Copy).then_inc(S["tt_ready"], 1)
            for c in range(2):
                act.wait_ge(S["cen2_full"], c + 1)
                nc.scalar.activation(sq[:, 4 * c:4 * c + 4, :], cen2[:, 4 * c:4 * c + 4, 0:P],
                                     ACT.Square).then_inc(S["sq2_ready"], 1)
            for i in range(4):
                c, b = divmod(i, 2)
                act.wait_ge(S["yt_full"], i + 1)
                nc.scalar.activation(yt2[:, b, c * NH:(c + 1) * NH], psum[:, YT_BANKS[i], :],
                                     ACT.Copy).then_inc(S["yt_ready"], 1)
                if i == 1:
                    act.wait_ge(S["delta_ready"], 1)
                    nc.scalar.activation(ed[:], dlt[:], ACT.Exp).then_inc(S["exp2_ready"], 1)
            act.wait_ge(S["gt_full"], 1)
            nc.scalar.activation(gate_t[:], psum[:, 2, :].bitcast(BF16), ACT.Copy).then_inc(S["gt_ready"], 1)

        @block.vector
        def _(dve):
            V = nc.vector
            chain = [0]

            def link(ins):
                chain[0] += 1
                ins.then_inc(S["dve_chain"], 1)
                dve.wait_ge(S["dve_chain"], chain[0])

            V.memset(qop[ZERO_FROM:MAX_ROW, 0, :, :].bitcast(U32), 0).then_inc(S["zeroed_q"], 1)
            for i in range(B * HALVES):
                b, hf = divmod(i, HALVES)
                cols_i = slice(hf * NH, (hf + 1) * NH)
                dve.wait_ge(S["part_h"], i + 1)
                V.scalar_tensor_tensor(out=rest[:, b, cols_i], in0=psum[:, 4 + i, :], scalar=cols_sb[:, 0:1],
                                       in1=part[0][:, b, cols_i], op0=ALU.add, op1=ALU.subtract).then_inc(S["part_r"], 1)
                dve.wait_ge(S["part_m"], i + 1)
                V.tensor_tensor(part[2][:, b, cols_i], rest[:, b, cols_i], part[1][:, b, cols_i],
                                ALU.subtract).then_inc(S["part_l"], 1)
            dve.wait_ge(S["v_full"], 1)
            dve.wait_ge(S["zeroed_v"], 1)
            dve.wait_ge(S["in_v"], 32)
            for t in range(TT):
                last = V.tensor_tensor(v_aug[:, t, :, :, 0:DH].rearrange("p b h d -> p (b h) d"),
                                       psum[:, 2 + t // 4, (t % 4) * P:(t % 4 + 1) * P].rearrange("p (h d) -> p h d", d=DH),
                                       bv_sb[:].rearrange("p (h d) -> p h d", d=DH), ALU.add)
            last.then_inc(S["v_ready"], 1)

            for r, (kind, blk, j, t) in enumerate(SLOT_JOBS):
                bank = 2 * (r % 2)
                b, g, hf = BLOCKS[blk]
                i = blk % 2
                dve.wait_ge(S["slot_full"], r + 1)
                if kind == "max":
                    if j == 0 and t == 0 and blk >= 2:
                        dve.wait_ge(S["max_split"], blk - 1)
                    V.tensor_reduce(negmax[:, i, j * QT + t:j * QT + t + 1],
                                    psum[:, bank:bank + 2, :].rearrange("p a n -> p (a n)"), AX_X, ALU.max,
                                    negate=True).then_inc(S["slot_free"], 1)
                elif kind == "max_t":
                    if blk >= 2:
                        dve.wait_ge(mrow_in[i], 16 * (blk // 2))
                    V.tensor_copy(max_row[:, i, :], psum[0:3 * HG * QT, bank, 0:P // 2].bitcast(BF16)
                                  ).then_inc(S["slot_free"], 1)
                else:
                    o = psum[:, bank, :].rearrange("p (t j v) -> p t j v", t=QT, j=HG)
                    link(V.reciprocal(rden[:, i, :, :], o[:, :, :, DH]))
                    dst = attn[:, hf * QT:(hf + 1) * QT, b, g * HG * DH:(g + 1) * HG * DH]
                    V.tensor_tensor(dst.rearrange("p t (j d) -> p t j d", j=HG), o[:, :, :, 0:DH],
                                    rden[:, i, :, :].rearrange("p t (j o) -> p t j o", o=1).broadcast_to([P, QT, HG, DH]),
                                    ALU.mult).then_inc(S["slot_free"], 1)

            dve.wait_ge(S["at_full"], 2)
            V.tensor_copy(attn_t[:, NH:], psum[:, 1, :]).then_inc(S["at_sb1"], 1)
            for c in range(2):
                dve.wait_ge(S["proj_ready"], c + 1)
                last = V.bn_stats(bn[:, c, :], proj[:, c * NH:(c + 1) * NH])
            link(last)
            V.bn_aggr(mv[:], bn[:].rearrange("p a b -> p (a b)")).then_inc(S["mean_ready"], 1)
            dve.wait_ge(S["mean_full"], 1)
            dve.wait_ge(S["mean_ready"], 1)
            link(V.tensor_copy(neg_mean[:], psum[:, 4, 0:1]))
            link(V.tensor_tensor(diff[:], mv[:, 0:1], neg_mean[:], ALU.add))
            V.scalar_tensor_tensor(out=dev[:], in0=diff[:], scalar=diff[:], in1=mv[:, 1:2], op0=ALU.mult,
                                   op1=ALU.add).then_inc(S["dev_ready"], 1)
            dve.wait_ge(S["var_full"], 1)
            V.tensor_scalar(gvar_eps[:], psum[:, 5, 0:1], EPS, None, ALU.add).then_inc(S["vareps_ready"], 1)
            dve.wait_ge(S["rstd_ready"], 1)
            link(V.tensor_tensor(gain[:], grstd[:], cols_sb[:, 2:3], ALU.mult))
            V.scalar_tensor_tensor(out=shift[:], in0=neg_mean[:], scalar=gain[:], in1=cols_sb[:, 3:4], op0=ALU.mult,
                                   op1=ALU.add).then_inc(S["aff_ready"], 1)
            for c in range(2):
                dve.wait_ge(S["affine_done"], c + 1)
                V.tensor_tensor(t1[:, c * NH:(c + 1) * NH], aff[:, c * NH:(c + 1) * NH], x_sb[:, c * NH:(c + 1) * NH],
                                ALU.add).then_inc(S["t1_ready"], 1)

            def rstd_of(c, norm):
                r = slice(8 * c, 8 * c + 8)
                link(V.tensor_reduce(ssq[:, r], sq[:, 4 * c:4 * c + 4, :].rearrange("p t (b c) -> p (t b) c", b=B), AX_X,
                                     ALU.add))
                V.tensor_scalar(var_eps[:, r], ssq[:, r], 1.0 / C, EPS, ALU.mult, ALU.add).then_inc(S["vareps_ready"], 1)
                dve.wait_ge(S["rstd_ready"], 2 + 2 * norm + c)
                return rstd[:, r].rearrange("p (t b o) -> p t b o", b=B, o=1)

            for c in range(2):
                dve.wait_ge(S["sq1_ready"], c + 1)
                r = rstd_of(c, 0)
                V.tensor_tensor(z[:, 4 * c:4 * c + 4, :].rearrange("p t (b c) -> p t b c", b=B),
                                psum[:, c, :].rearrange("p (t b c) -> p t b c", b=B, c=C),
                                r.broadcast_to([P, 4, B, C]), ALU.mult).then_inc(S["z_ready"], 1)
            dve.wait_ge(S["gram0_full"], 1)
            V.tensor_tensor(gram[:], psum[:, 6, 0:P], diag_mask, ALU.mult).then_inc(S["gram_ready"], 1)
            for l in range(LAYERS):
                dve.wait_ge(S["gv_full"], 2 * l + 2)
                V.tensor_copy(gv[:, NHEAD // 2:, :],
                              psum[:, 5, 0:NHEAD * C // 2].rearrange("p (j c) -> p j c", c=C)).then_inc(S["gv_dve"], 1)
                dve.wait_ge(S["m_full"], l + 1)
                V.scalar_tensor_tensor(out=w_l[:], in0=psum[:, 4, 0:P], scalar=1.0 / (N * NHEAD), in1=diag_mask,
                                       op0=ALU.mult, op1=ALU.mult).then_inc(S["w_ready"], 1)
                if l < LAYERS - 1:
                    dve.wait_ge(S["u_full"], l + 1)
                    V.tensor_copy(u_l[:], psum[:, 6, 0:P]).then_inc(S["u_ready"], 1)
                    dve.wait_ge(S["gram_full"], l + 1)
                    V.tensor_copy(gram[:], psum[:, 5, 0:P]).then_inc(S["gram_ready"], 1)
            for c in range(2):
                dve.wait_ge(S["attn2_full"], c + 1)
                V.tensor_tensor(t2[:, c * NH:(c + 1) * NH], psum[:, c, :], t1[:, c * NH:(c + 1) * NH],
                                ALU.add).then_inc(S["t2_ready"], 1)
            for c in range(2):
                dve.wait_ge(S["sq2_ready"], c + 1)
                r = rstd_of(c, 1)
                for dup in range(2):
                    last = V.tensor_tensor(y[:, 4 * c:4 * c + 4, :, dup, :],
                                           cen2[:, 4 * c:4 * c + 4, 0:P].rearrange("p t (b c) -> p t b c", b=B),
                                           r.broadcast_to([P, 4, B, C]), ALU.mult)
                last.then_inc(S["y_ready"], 1)

            G16 = TT * B

            def over_e(v):
                return v[:].rearrange("p (a o) -> p a o", o=1).broadcast_to([P, G16, E])

            def over_tokens(v):
                return v[:].rearrange("p (o e) -> p o e", o=1).broadcast_to([P, G16, E])

            dve.wait_ge(S["in_rest"], 16 * IN_REST)
            V.tensor_tensor(lg[:].rearrange("p (t b) e -> p t b e", b=B),
                            cen2[:, :, P:P + B * E].rearrange("p t (b e) -> p t b e", b=B),
                            rstd[:].rearrange("p (t b o) -> p t b o", b=B, o=1).broadcast_to([P, TT, B, E]),
                            ALU.mult).then_inc(S["logits_read"], 1)
            dve.wait_ge(S["logits_read"], 1)
            link(V.tensor_tensor(lg[:], lg[:], over_tokens(rb_sb), ALU.add))

            def one_hot_of_largest(logits, largest, hot):
                link(V.tensor_reduce(largest[:], logits[:], AX_X, ALU.max))
                link(V.tensor_tensor(cand[:], logits[:], over_e(largest), ALU.is_equal))
                link(V.tensor_tensor(cand[:], cand[:], over_tokens(weight_sb), ALU.mult))
                link(V.tensor_reduce(pick[:], cand[:], AX_X, ALU.max))
                link(V.tensor_tensor(hot[:], over_tokens(weight_sb), over_e(pick), ALU.is_equal))

            one_hot_of_largest(lg, m1, hot1)
            link(V.scalar_tensor_tensor(out=lg2[:], in0=hot1[:], scalar=-3e38, in1=lg[:], op0=ALU.mult, op1=ALU.add))
            one_hot_of_largest(lg2, m2, hot2)
            V.tensor_tensor(dlt[:], m2[:], m1[:], ALU.subtract).then_inc(S["delta_ready"], 1)
            dve.wait_ge(S["exp2_ready"], 1)
            link(V.tensor_scalar(gate1[:], ed[:], 1.0, None, ALU.add))
            link(V.reciprocal(gate1[:], gate1[:]))
            link(V.tensor_tensor(gate2[:], ed[:], gate1[:], ALU.mult))
            link(V.tensor_tensor(hot1[:], hot1[:], over_e(gate1), ALU.mult))
            link(V.tensor_tensor(hot2[:], hot2[:], over_e(gate2), ALU.mult))
            link(V.tensor_tensor(gates[:], hot1[:], hot2[:], ALU.add))
            dve.wait_ge(S["gate_zeroed"], 1)
            gp = [gate_part[:, :, s * B * E:(s + 1) * B * E] for s in range(3)]
            gf = gates[:].rearrange("p (t b) e -> p t (b e)", b=B)
            gr = gate_rest[:].rearrange("p (t b) e -> p t (b e)", b=B)
            link(V.tensor_copy(gp[0], gf))
            link(V.tensor_tensor(gr, gf, gp[0], ALU.subtract))
            link(V.tensor_copy(gp[1], gr))
            V.tensor_tensor(gp[2], gr, gp[1], ALU.subtract).then_inc(S["gate_split"], 1)
            for i, (c, b, k) in enumerate(MOE):
                dve.wait_ge(S["gb_full"], i + 1)
                if i >= 4:
                    dve.wait_ge(S["moe_done"], i - 3)
                V.tensor_tensor(scaled[:, i % 4, :], psum[:, GB_BANKS[i % len(GB_BANKS)], :],
                                yt2[:, b, c * NH:(c + 1) * NH], ALU.mult).then_inc(S["scaled_ready"], 1)
                if i == len(MOE) // 2 + GB_LAG:
                    dve.wait_ge(S["moe_done"], len(MOE) // 2)
                    V.tensor_tensor(res[:, 0:NH], psum[:, MOE_BANKS[0], :], t2[:, 0:NH], ALU.add).then_inc(S["out_done"], 1)
            dve.wait_ge(S["moe_done"], len(MOE))
            V.tensor_tensor(res[:, NH:], psum[:, MOE_BANKS[1], :], t2[:, NH:], ALU.add).then_inc(S["out_done"], 1)


def kernel(**inputs):
    import numpy as np
    import concourse.bacc as bacc
    from concourse.bass_utils import run_bass_kernel_spmd

    f32 = np.float32
    get = {k.removeprefix("L0_conv_").removeprefix("L1_"): np.asarray(v, f32) for k, v in inputs.items()}

    def diag(a, n=B):
        out = np.zeros((n * a.shape[0], n * a.shape[1]), a.dtype)
        for i in range(n):
            out[i * a.shape[0]:(i + 1) * a.shape[0], i * a.shape[1]:(i + 1) * a.shape[1]] = a
        return out

    x = get["x"].reshape(P, N)

    def by_channel(q, k):
        return np.stack([q, k]).reshape(2, H, DH, -1).transpose(2, 0, 1, 3).reshape(P, -1)

    qk = by_channel(get["Wq"], get["Wk"]).T
    wqk = np.zeros((P, B, P), f32)
    for b in range(B):
        wqk[b * C:(b + 1) * C, b] = qk
    cols = np.stack([by_channel(get["bq"], get["bk"])[:, 0]] + [np.tile(get[n], B) for n in ("bo", "gn_w", "gn_b")], 1)
    bv_row = np.broadcast_to(np.tile(get["bv"], B), (P, P))
    v, q = get["attn_v_matrix"][:, :, 0], get["attn_q_matrix"][:, :, 0]
    vt = np.tile(v.transpose(3, 0, 1, 2).reshape(C, LAYERS, NHEAD * C), (B, 1, 1))
    qt = np.zeros((P, LAYERS * NHEAD, P), f32)
    for b in range(B):
        qt[b * C:(b + 1) * C, :, b * C:(b + 1) * C] = q.transpose(3, 0, 1, 2).reshape(C, LAYERS * NHEAD, C)
    cen_r = diag(get["ffn_router_w"])
    expw = get["ffn_expert_w"].reshape(E // 2, 2 * C, C).transpose(1, 0, 2)
    expb = np.zeros((P, P), f32)
    expb[:3 * B * E] = np.tile(diag(get["ffn_expert_b"]), (3, 1))
    rb_row = np.broadcast_to(get["ffn_router_b"], (P, E))

    eye = np.eye(P, dtype=f32)
    group = C // 8
    avg = np.kron(np.eye(P // group), np.full((group, group), 1.0 / group)).astype(f32)
    centre = eye - diag(np.full((C, C), 1.0 / C, f32))
    consts = np.concatenate([eye, centre, -avg, avg, diag(np.ones((C, C), f32)), eye * (N * NHEAD),
                             np.broadcast_to(np.arange(E, 0, -1, dtype=f32), (P, E))], 1)
    select = np.zeros((P, B * E // 2, P), f32)
    for s in range(3):
        for b in range(B):
            for e in range(E):
                select[(s * B + b) * E + e, b * (E // 2) + e // 2, (e % 2) * C:(e % 2 + 1) * C] = 1
    from concourse import mybir as mb
    bf = mb.dt.np(mb.dt.bfloat16) if hasattr(mb.dt, "np") else None
    import ml_dtypes
    bf = ml_dtypes.bfloat16
    cbf = np.concatenate([eye.astype(bf), select.reshape(P, -1).astype(bf)], 1)
    ones = np.ones((3, B, H, N), bf)

    nc = bacc.Bacc("TRN2", target_bir_lowering=False, num_devices=1)
    arrays, args = {}, []
    for name, a in dict(x=x, wqk=wqk, wv=diag(get["Wv"].T.copy()), wo=diag(get["Wo"].T.copy()), cols=cols, bv_row=bv_row, vt=vt,
                        qt=qt, router=cen_r, expw=expw, expb=expb, rb_row=rb_row, consts=consts, cbf=cbf,
                        ones=ones).items():
        a = np.ascontiguousarray(a)
        arrays[f"in_{name}"] = a
        args.append(nc.dram_tensor(f"in_{name}", a.shape, mybir.dt.from_np(a.dtype), kind="ExternalInput").ap())
    args.append(nc.dram_tensor("out", (P, N), F32, kind="ExternalOutput").ap())
    conv_attn_hybrid_kernel(nc, *args)
    r = run_bass_kernel_spmd(nc, [arrays], core_ids=[0])
    return r.results[0]["out"].reshape(B, C, 32, 32)
```

```python
from contextlib import ExitStack

import concourse.bass as bass
from concourse import mybir

ALU = mybir.AluOpType
ACT = mybir.ActivationFunctionType
AX_X = mybir.AxisListType.X
F32 = mybir.dt.float32
BF16 = mybir.dt.bfloat16
U32 = mybir.dt.uint32

P = 128
B = 2
C = 64
N = 1024
H = 8
DH = C // H
HG = 4
NG = H // HG
NH = 512
HALVES = N // NH
TT = N // P
QB = 256
QT = QB // P
BLOCKS = [(b, g, qb) for b in range(B) for g in range(NG) for qb in range(N // QB)]
UNITS = TT * len(BLOCKS)
PAIRS = HG // 2
VW = 32
LAYERS = 4
NHEAD = 8
E = 8
SCALE = float(DH) ** -0.5
EPS = 1e-5

PARTS = 3
STORED = PARTS + 2
PART_ROWS = DH * PARTS
ZERO_FROM = 64
MAX_ROW = 96
SCORE_ROWS = MAX_ROW + 3

WARM_COLS = 256
LEAD = 15
PV_LAG = 3
ST_BANKS = (4, 5, 6)
PV_BANK = 7
P_RING = 8
IN_REST = 10
PROJ_BANKS = (1, 3)
CEN_BANKS = (0, 2)
YT_BANKS = (6, 7, 0, 1)
GT_BANKS = (2, 5)
GB_BANKS = (3, 4, 5, 0, 1)
MOE_BANKS = (6, 7)
GB_LAG = 4
MOE = [(c, b, k) for c in range(2) for k in range(E // 2) for b in range(B)]
BY_POOL = [i for i in range(len(MOE)) if i % 3 == 1]
BY_DVE = [i for i in range(len(MOE)) if i not in BY_POOL]
SCALED = 6


def conv_attn_hybrid_kernel(nc, x, wqk, wv, wo, cols, bv_row, vt, q_pairs, router, expw, expb, rb_row, consts, cbf, ones, out):
    with ExitStack() as ctx:
        def sb(name, shape, dt=F32):
            return ctx.enter_context(nc.sbuf_tensor(name, shape, dt))

        def sem(name):
            return ctx.enter_context(nc.semaphore(name))

        parts_dram = nc.dram_tensor("parts_scratch", (B, STORED, P, N), BF16, kind="Internal").ap()
        max_dram = nc.dram_tensor("max_scratch", (len(BLOCKS), 3 * HG * QT, P), BF16, kind="Internal").ap()
        psum = ctx.enter_context(nc.psum_tensor("psum", [P, 8, 512], F32))

        cen2 = psum[:, 2:6, :].rearrange("p a (h n) -> p (a h) n", h=2)

        x_sb = sb("x_sb", [P, N])
        wqk_sb = sb("wqk_sb", [P, B, P])
        wv_sb = sb("wv_sb", [P, P])
        wo_sb = sb("wo_sb", [P, P])
        cols_sb = sb("cols_sb", [P, 4])
        bv_sb = sb("bv_sb", [P, P])
        vt_sb = sb("vt_sb", [P, LAYERS, 2, NHEAD // 2 * C])
        q_pair = sb("q_pair", [P, LAYERS, NHEAD // 2, C])
        rw_sb = sb("rw_sb", [P, B * E])
        expw_sb = sb("expw_sb", [P, E // 2, C])
        expb_sb = sb("expb_sb", [P, P])
        rb_sb = sb("rb_sb", [P, E])
        consts_sb = sb("consts_sb", [P, 6, P])
        eye2_sb = sb("eye2_sb", [P, C])
        ident, centre, neg_avg, avg, diag_mask, ident_n = (consts_sb[:, i, :] for i in range(6))
        weight_sb = sb("weight_sb", [P, E])
        cbf_sb = sb("cbf_sb", [P, 1 + B * E // 2, P], BF16)
        ident_bf = cbf_sb[:, 0, :]
        select = cbf_sb[:, 1:, :]

        part = [sb(f"part{i}", [P, B, N], BF16) for i in range(3)]
        rest = sb("rest", [P, B, N])
        warm = sb("warm", [P, 2])
        qop = sb("qop", [P, B, H, N], BF16)
        kop = sb("kop", [P, B, H, N], BF16)
        v_aug = sb("v_aug", [P, TT, B, H, VW])
        negmax_half = sb("negmax_half", [P, 2, HALVES, HG * QT])
        negmax = sb("negmax", [P, 2, HG * QT])
        max_rest = sb("max_rest", [P, 2, HG * QT])
        max_part = sb("max_part", [P, 2, 3, HG * QT], BF16)
        max_row = sb("max_row", [3 * HG * QT, 2, P], BF16)
        probs = sb("probs", [P, P_RING, HG, QB])
        o_sb = sb("o_sb", [P, 2, QB])
        rden = sb("rden", [P, 2, QT, HG])
        attn = sb("attn", [P, TT, B, C])

        spare_q = qop[:].rearrange("p b h n -> p (b h n)").bitcast(F32)
        y = spare_q[:, 0:2 * N].rearrange("p (t b u c) -> p t b u c", t=TT, b=B, u=2)
        yt2 = spare_q[:, 2 * N:4 * N].rearrange("p (b n) -> p b n", b=B)
        res = spare_q[:, 4 * N:5 * N]
        scaled = spare_q[:, 5 * N:5 * N + SCALED * NH].rearrange("p (i n) -> p i n", n=NH)
        spare = probs[:].rearrange("p u j n -> p (u j n)").rearrange("p (a n) -> p a n", n=N)
        aff, t1, z_t, t2 = (spare[:, i, :] for i in range(4))
        gate_copy = spare[:, 4, :].rearrange("p (i n) -> p i n", n=NH)
        z, sq = (spare[:, i, :].rearrange("p (t c) -> p t c", c=P) for i in (6, 7))
        attn_t = sb("attn_t", [P, N])
        bn = sb("bn", [P, 2, 6])
        mv = sb("mv", [P, 2])
        neg_mean, mean_b, diff, dev, grstd, gain, shift = (sb(n, [P, 1]) for n in ("neg_mean", "mean_b", "diff", "dev", "grstd", "gain", "shift"))
        ssq = sb("ssq", [P, TT * B])
        rstd = sb("rstd", [P, TT * B])
        var_eps = sb("var_eps", [P, TT * B])
        root = sb("root", [P, TT * B])
        newton = sb("newton", [P, TT * B])
        gram = sb("gram", [P, P])
        gv = sb("gv", [P, B, NHEAD // 2, C])
        w_l = sb("w_l", [P, P])
        u_l = sb("u_l", [P, P])
        tt_l = sb("tt_l", [P, P])
        tt_f = sb("tt_f", [P, P])
        cen_rw = sb("cen_rw", [P, P + B * E])
        lg = sb("lg", [P, TT * B, E])
        lg2 = sb("lg2", [P, TT * B, E])
        m1 = sb("m1", [P, TT * B])
        m2 = sb("m2", [P, TT * B])
        cand = sb("cand", [P, TT * B, E])
        pick = sb("pick", [P, TT * B])
        hot1 = sb("hot1", [P, TT * B, E])
        hot2 = sb("hot2", [P, TT * B, E])
        dlt = sb("dlt", [P, TT * B])
        ed = sb("ed", [P, TT * B])
        gate1 = sb("gate1", [P, TT * B])
        gate2 = sb("gate2", [P, TT * B])
        gates = sb("gates", [P, TT * B, E])
        gate_rest = sb("gate_rest", [P, TT * B, E])
        gate_part = sb("gate_part", [P, TT, P], BF16)
        gate_t = sb("gate_t", [P, N], BF16)
        expb_part = sb("expb_part", [P, 3, P], BF16)
        expb_rest = sb("expb_rest", [P, P])

        names = (
            "warm in_x in_qk in_c in_v in_ident in_rest zeroed_q zeroed_q1 zeroed_k zeroed_v v_ready qk_full part_h part_r part_m part_l v_full "
            "slot_full slot_free st_full exp_done pv_done o_copied out_written pool_chain max_ready max_split max_out "
            "dve_chain proj_full crw_full crw_ready mean_ready mean_full dev_ready var_full "
            "aff_ready affine_done t1_ready cen1_full sq1_ready z_ready gram0_full zt_full zt_ready gv_full gv_act gv_dve "
            "m_full w_ready u_full u_ready tt_full tt_ready gram_full gram_ready attn2_full t2_ready cen2_full sq2_ready "
            "y_ready yt_full yt_ready logits_read delta_ready exp2_ready gates_ready gate_zeroed gate_split gt_full "
            "gt_ready var_ready root_ready rstd_ready gt_ready2 gb_full gb_copied scaled_dve scaled_pool moe_done out_done expb_split").split()
        S = {n: sem(n) for n in names}
        ops_ready = [[sem(f"ops_ready{b}{g}") for g in range(NG)] for b in range(B)]
        mrow_in = [sem(f"mrow_in{i}") for i in range(2)]
        N_OPS = 2 * PARTS
        parts_out = [sem(f"parts_out{b}") for b in range(B)]

        jobs_at = {}
        EARLY = TT * (len(BLOCKS) - 2) + PV_LAG + 3
        for u in range(-LEAD, UNITS + 8):
            v = u + LEAD
            jobs = []
            if 0 <= v < UNITS:
                blk, k = divmod(v, TT)
                jobs += [("max", blk, k, c) for c in range(HALVES)]
            if v >= TT + 2 and (v - 2) % TT == 0 and (v - 2) // TT <= len(BLOCKS):
                jobs.append(("max_t", (v - 2) // TT - 1, 0, 0))
            w = u - PV_LAG - 1
            if w >= TT and w % TT == 0 and w // TT <= len(BLOCKS):
                jobs.append(("out_t", w // TT - 1, 0, 0))
            if u == EARLY:
                jobs.append(("attn_t", 0, 0, 0))
            if u == UNITS + PV_LAG + 2:
                jobs.append(("attn_t", 1, 0, 0))
            jobs_at[u] = jobs
        SLOT_JOBS = [j for u in range(-LEAD, UNITS + 8) for j in jobs_at[u]]

        LAST_MAX = max(r for r, job in enumerate(SLOT_JOBS) if job[0] == "max")
        slot_bank = [r % 4 if r <= LAST_MAX else 2 * (r % 2) for r in range(len(SLOT_JOBS))]

        def bank_free_at(r):
            return max([p for p in range(r) if slot_bank[p] == slot_bank[r]], default=-1) + 1

        def jobs_until(kind, blk):
            return max(r for r, job in enumerate(SLOT_JOBS) if job[:2] == (kind, blk)) + 1

        block = ctx.enter_context(nc.Block())

        @block.sync
        def _(sp):
            sp.dma_start(x_sb[:], x).then_inc(S["in_x"], 16)
            sp.dma_start(cols_sb[:], cols).then_inc(S["in_qk"], 16)
            sp.dma_start(wqk_sb[:], wqk).then_inc(S["in_qk"], 16)
            sp.dma_start(wv_sb[:], wv).then_inc(S["in_v"], 16)
            sp.dma_start(bv_sb[:], bv_row).then_inc(S["in_v"], 16)
            sp.dma_start(cbf_sb[:], cbf.rearrange("p (a n) -> p a n", n=P)).then_inc(S["in_c"], 16)
            sp.dma_start(kop[MAX_ROW:SCORE_ROWS, :, :, :], ones).then_inc(S["in_c"], 16)
            sp.wait_ge(S["zeroed_q"], 1)
            sp.wait_ge(S["zeroed_k"], 1)
            def store_parts(b):
                for i, name in enumerate(("part_h", "part_m", "part_l")):
                    sp.wait_ge(S[name], HALVES * (b + 1))
                    for stored in range(i, STORED, PARTS):
                        sp.dma_start(parts_dram[b, stored, :, :], part[i][:, b, :]).then_inc(parts_out[b], 16)

            def operands(b, g):
                sp.wait_ge(parts_out[b], 16 * STORED)
                sp.wait_ge(S["zeroed_k"], b + 1)
                sp.wait_ge(S["zeroed_q1" if b else "zeroed_q"], 1)
                rows = parts_dram[b].rearrange("s (d w h) n -> (s d) w (h n)", d=DH, w=2)
                at_g = slice(g * HG * N, (g + 1) * HG * N)
                for r in range(PARTS):
                    to = slice(r * PART_ROWS, (r + 1) * PART_ROWS)
                    sp.dma_start(qop[to, b, g * HG:(g + 1) * HG, :],
                                 rows[0:PART_ROWS, 0, at_g]).then_inc(ops_ready[b][g], 16)
                    sp.dma_start(kop[to, b, g * HG:(g + 1) * HG, :],
                                 rows[r * DH:r * DH + PART_ROWS, 1, at_g]).then_inc(ops_ready[b][g], 16)

            def max_rows(i):
                b, g, qb = BLOCKS[i]
                sp.wait_ge(S["slot_free"], jobs_until("max_t", i))
                sp.dma_start(max_dram[i], max_row[:, i % 2, :]).then_inc(S["max_out"], 16)
                sp.wait_ge(S["max_out"], 16 * (i + 1))
                sp.dma_start(qop[MAX_ROW:SCORE_ROWS, b, g * HG:(g + 1) * HG, qb * QB:(qb + 1) * QB],
                             max_dram[i].rearrange("(s j t) n -> s j (t n)", s=PARTS, j=HG)).then_inc(mrow_in[i % 2], 16)

            store_parts(0)
            operands(0, 0)
            max_rows(0)
            operands(0, 1)
            max_rows(1)
            sp.dma_start(consts_sb[:], consts[:, 0:6 * P].rearrange("p (a n) -> p a n", n=P)).then_inc(S["in_ident"], 16)
            store_parts(1)
            max_rows(2)
            operands(1, 0)
            max_rows(3)
            operands(1, 1)
            max_rows(4)
            for at, source in ((weight_sb[:], consts[:, 6 * P:6 * P + E]), (cen_rw[:, 0:P], consts[:, P:2 * P]),
                               (rw_sb[:], router), (wo_sb[:], wo), (expw_sb[:], expw), (expb_sb[:], expb),
                               (rb_sb[:], rb_row),
                               (eye2_sb[:], consts[:, 6 * P + E:])):
                sp.dma_start(at, source).then_inc(S["in_rest"], 16)
            max_rows(5)
            sp.dma_start(vt_sb[:], vt).then_inc(S["in_rest"], 16)
            sp.dma_start(q_pair[:], q_pairs).then_inc(S["in_rest"], 16)
            for i in range(6, len(BLOCKS)):
                max_rows(i)
            for c in range(2):
                sp.wait_ge(S["out_done"], c + 1)
                sp.dma_start(out[:, c * NH:(c + 1) * NH], res[:, c * NH:(c + 1) * NH]).then_inc(S["out_written"], 16)
            sp.wait_ge(S["out_written"], 32)

        @block.tensor
        def _(pe):
            pe.wait_ge(S["in_x"], 16)
            pe.wait_ge(S["in_qk"], 32)
            for i in range(B * HALVES):
                b, hf = divmod(i, HALVES)
                nc.tensor.matmul(psum[:, 4 + i, :], wqk_sb[:, b, :], x_sb[:, hf * NH:(hf + 1) * NH],
                                 start=True, stop=True).then_inc(S["qk_full"], 1)
            pe.wait_ge(S["in_v"], 32)
            for t in range(TT):
                last = nc.tensor.matmul(psum[:, 2 + t // 4, (t % 4) * P:(t % 4 + 1) * P], x_sb[:, t * P:(t + 1) * P],
                                        wv_sb[:], start=True, stop=True, skip_group_check=True)
            last.then_inc(S["v_full"], 1)

            slot = [0]

            def fill_slot(job):
                kind, blk, k, c = job
                r = slot[0]
                slot[0] += 1
                bank = slot_bank[r]
                if bank_free_at(r):
                    pe.wait_ge(S["slot_free"], bank_free_at(r))
                b, g, qb = BLOCKS[blk]
                if kind == "max":
                    if k == 0 and c == 0:
                        pe.wait_ge(ops_ready[b][g], 16 * N_OPS)
                    if r == 2:
                        pe.wait_ge(S["v_ready"], 1)
                    j, t = divmod(k, QT)
                    last = nc.tensor.matmul(psum[:, bank, :],
                                            qop[0:MAX_ROW, b, g * HG + j, qb * QB + t * P:qb * QB + (t + 1) * P],
                                            kop[0:MAX_ROW, b, g * HG + j, c * NH:(c + 1) * NH], start=True, stop=True)
                elif kind == "max_t":
                    pe.wait_ge(S["max_split"], blk + 1)
                    pe.wait_ge(S["in_c"], 32)
                    dst = psum[0:3 * HG * QT, bank, 0:P // 2].bitcast(BF16)
                    last = nc.tensor.transpose(dst, max_part[:, blk % 2, :, :], ident_bf)
                elif kind == "attn_t":
                    pe.wait_ge(S["slot_free"], r)
                    for q in range(TT // 2):
                        last = nc.tensor.transpose(psum[:, bank, q * P:(q + 1) * P],
                                                   attn[:, blk * TT // 2 + q, :, :], ident)
                else:
                    pe.wait_ge(S["o_copied"], blk + 1)
                    pe.wait_ge(S["in_ident"], 16)
                    for q in range(QT):
                        last = nc.tensor.transpose(psum[:, bank, q * P:(q + 1) * P],
                                                   o_sb[:, blk % 2, q * P:(q + 1) * P], ident)
                last.then_inc(S["slot_full"], 1)

            def scores(u, pair):
                blk, mt = divmod(u, TT)
                b, g, qb = BLOCKS[blk]
                s = PAIRS * u + pair
                if mt == 0 and pair == 0:
                    pe.wait_ge(mrow_in[blk % 2], 16 * (blk // 2 + 1))
                if s >= len(ST_BANKS):
                    pe.wait_ge(S["exp_done"], s - len(ST_BANKS) + 1)
                elif s == 0:
                    pe.wait_ge(S["in_c"], 32)
                    pe.wait_ge(S["part_r"], B * HALVES)
                for i in range(2):
                    h = g * HG + 2 * pair + i
                    last = nc.tensor.matmul(psum[:, ST_BANKS[s % len(ST_BANKS)], i * QB:(i + 1) * QB],
                                            kop[0:SCORE_ROWS, b, h, mt * P:(mt + 1) * P],
                                            qop[0:SCORE_ROWS, b, h, qb * QB:(qb + 1) * QB],
                                            start=True, stop=True, skip_group_check=True)
                last.then_inc(S["st_full"], 1)

            def values(u):
                blk, mt = divmod(u, TT)
                b, g, qb = BLOCKS[blk]
                pe.wait_ge(S["exp_done"], PAIRS * (u + 1))
                if mt == 0 and blk:
                    pe.wait_ge(S["o_copied"], blk)
                if u == 0:
                    pe.wait_ge(S["v_ready"], 1)
                for j in range(HG):
                    last = nc.tensor.matmul(psum[j * VW:(j + 1) * VW, PV_BANK, 0:QB], v_aug[:, mt, b, g * HG + j, :],
                                            probs[:, u % P_RING, j, :], start=mt == 0, stop=mt == TT - 1,
                                            skip_group_check=True)
                last.then_inc(S["pv_done"], 1)

            def keep_warm(n, bank):
                for _ in range(n):
                    nc.tensor.matmul(psum[:, bank, 0:WARM_COLS], ident_bf, cbf_sb[:, 1:1 + WARM_COLS // P, :],
                                     start=True, stop=True, skip_group_check=True)

            def project(c):
                pe.wait_ge(S["slot_free"], jobs_until("attn_t", c))
                if c == 0:
                    pe.wait_ge(S["in_rest"], 16 * IN_REST)
                nc.tensor.matmul(psum[:, PROJ_BANKS[c], :], wo_sb[:], attn_t[:, c * NH:(c + 1) * NH],
                                 start=True, stop=True).then_inc(S["proj_full"], 1)

            for u in range(-LEAD, UNITS + 8):
                jobs = list(jobs_at[u])
                if u == EARLY + 2:
                    project(0)
                v = u - PV_LAG
                if 0 <= u < UNITS:
                    scores(u, 0)
                if 0 < v - 1 < UNITS and (v - 1) % TT == 0:
                    values(v - 1)
                for job in jobs[:HALVES]:
                    fill_slot(job)
                if 0 <= u < UNITS:
                    scores(u, 1)
                for job in jobs[HALVES:]:
                    fill_slot(job)
                if 0 <= v < UNITS and (v == 0 or v % TT):
                    values(v)

            keep_warm(6, PV_BANK)
            project(1)
            nc.tensor.matmul(psum[:, 6, 0:B * E], centre, rw_sb[:], start=True, stop=True).then_inc(S["crw_full"], 1)
            keep_warm(10, PV_BANK)
            pe.wait_ge(S["mean_ready"], 1)
            nc.tensor.matmul(psum[:, 4, 0:1], neg_avg, mean_b[:], start=True, stop=True).then_inc(S["mean_full"], 1)
            keep_warm(7, PV_BANK)
            pe.wait_ge(S["dev_ready"], 1)
            nc.tensor.matmul(psum[:, 5, 0:1], avg, dev[:], start=True, stop=True).then_inc(S["var_full"], 1)
            keep_warm(22, PV_BANK)
            for c in range(2):
                pe.wait_ge(S["t1_ready"], c + 1)
                for t in range(4 * c, 4 * c + 4):
                    last = nc.tensor.matmul(psum[:, CEN_BANKS[c], (t % 4) * P:(t % 4 + 1) * P], t1[:, t * P:(t + 1) * P], centre,
                                            start=True, stop=True, skip_group_check=True)
                last.then_inc(S["cen1_full"], 1)
            keep_warm(22, PV_BANK)
            for c in range(2):
                pe.wait_ge(S["z_ready"], c + 1)
                for t in range(4 * c, 4 * c + 4):
                    last = nc.tensor.matmul(psum[:, 6, 0:P], z[:, t, :], z[:, t, :], start=t == 0, stop=t == TT - 1)
            last.then_inc(S["gram0_full"], 1)
            for c in range(2):
                for t in range(4 * c, 4 * c + 4):
                    last = nc.tensor.transpose(psum[:, PROJ_BANKS[c], (t % 4) * P:(t % 4 + 1) * P], z[:, t, :], ident)
                last.then_inc(S["zt_full"], 1)
            for l in range(LAYERS):
                pe.wait_ge(S["gram_ready"], l + 1)
                if l:
                    pe.wait_ge(S["tt_ready"], l)
                for b in range(B):
                    for odd in range(2):
                        last = nc.tensor.matmul(psum[odd * C:(odd + 1) * C, (7, 5)[b], 0:NHEAD // 2 * C],
                                                gram[:, b * C:(b + 1) * C], vt_sb[:, l, odd, :],
                                                start=True, stop=True, skip_group_check=True)
                    last.then_inc(S["gv_full"], 1)
                nc.tensor.matmul(psum[:, 4, 0:C], ident_n, eye2_sb[:], start=True, stop=False, skip_group_check=True)
                for b in range(B):
                    pe.wait_ge(S[("gv_act", "gv_dve")[b]], l + 1)
                    for k in range(NHEAD // 2):
                        last = nc.tensor.matmul(psum[b * C:(b + 1) * C, 4, 0:C], q_pair[:, l, k, :], gv[:, b, k, :],
                                                start=False, stop=k == NHEAD // 2 - 1, skip_group_check=True)
                last.then_inc(S["m_full"], 1)
                pe.wait_ge(S["w_ready"], l + 1)
                if l < LAYERS - 1:
                    nc.tensor.matmul(psum[:, 6, 0:P], gram[:], w_l[:], start=True, stop=True).then_inc(S["u_full"], 1)
                    nc.tensor.matmul(psum[:, 7, 0:P], w_l[:], tt_l[:] if l else ident,
                                     start=True, stop=True).then_inc(S["tt_full"], 1)
                    pe.wait_ge(S["u_ready"], l + 1)
                    nc.tensor.matmul(psum[:, 5, 0:P], w_l[:], u_l[:], start=True, stop=True).then_inc(S["gram_full"], 1)
                else:
                    nc.tensor.matmul(psum[:, 7, 0:P], tt_l[:], w_l[:], start=True, stop=True).then_inc(S["tt_full"], 1)
            pe.wait_ge(S["tt_ready"], LAYERS)
            pe.wait_ge(S["zt_ready"], 2)
            for c in range(2):
                nc.tensor.matmul(psum[:, c, :], tt_f[:], z_t[:, c * NH:(c + 1) * NH],
                                 start=True, stop=True).then_inc(S["attn2_full"], 1)
            pe.wait_ge(S["crw_ready"], 1)
            for c in range(2):
                pe.wait_ge(S["t2_ready"], c + 1)
                for t in range(4 * c, 4 * c + 4):
                    last = nc.tensor.matmul(cen2[:, t, 0:P + B * E], t2[:, t * P:(t + 1) * P], cen_rw[:],
                                            start=True, stop=True, skip_group_check=True)
                last.then_inc(S["cen2_full"], 1)
            keep_warm(44, YT_BANKS[3])
            for c in range(2):
                if c:
                    keep_warm(10, YT_BANKS[3])
                pe.wait_ge(S["y_ready"], TT * B // 2 * (c + 1))
                for b in range(B):
                    for t in range(4 * c, 4 * c + 4):
                        last = nc.tensor.transpose(psum[:, YT_BANKS[2 * c + b], (t % 4) * P:(t % 4 + 1) * P],
                                                   y[:, t, b, :, :], ident)
                    last.then_inc(S["yt_full"], 1)
            keep_warm(3, GB_BANKS[0])
            pe.wait_ge(S["logits_read"], 1)
            for c in range(2):
                pe.wait_ge(S["gate_split"], c + 1)
                for t in range(TT // 2):
                    last = nc.tensor.transpose(psum[:, GT_BANKS[c], t * P // 2:(t + 1) * P // 2].bitcast(BF16),
                                               gate_part[:, c * TT // 2 + t, :], ident_bf)
                last.then_inc(S["gt_full"], 1)
            pe.wait_ge(S["gt_ready"], 1)
            pe.wait_ge(S["gt_ready2"], 1)
            pe.wait_ge(S["expb_split"], 1)
            pe.wait_ge(S["yt_ready"], 4)
            for i in range(len(MOE) + GB_LAG):
                if i < len(MOE):
                    c, b, k = MOE[i]
                    r = i - len(GB_BANKS)
                    if r in BY_DVE:
                        pe.wait_ge(S["scaled_dve"], BY_DVE.index(r) + 1)
                    elif r >= 0:
                        pe.wait_ge(S["gb_copied"], BY_POOL.index(r) + 1)
                    nc.tensor.matmul(psum[:, GB_BANKS[i % len(GB_BANKS)], :], select[:, b * (E // 2) + k, :],
                                     gate_t[:, c * NH:(c + 1) * NH], start=True, stop=True).then_inc(S["gb_full"], 1)
                r = i - GB_LAG
                if r >= 0:
                    c, b, k = MOE[r]
                    if b == 0 and k == 0:
                        for s in range(3):
                            nc.tensor.matmul(psum[:, MOE_BANKS[c], :], expb_part[:, s, :],
                                             gate_t[:, c * NH:(c + 1) * NH], start=s == 0, stop=False,
                                             skip_group_check=True)
                    if r in BY_DVE:
                        pe.wait_ge(S["scaled_dve"], BY_DVE.index(r) + 1)
                    else:
                        pe.wait_ge(S["scaled_pool"], BY_POOL.index(r) + 1)
                    nc.tensor.matmul(psum[b * C:(b + 1) * C, MOE_BANKS[c], :], expw_sb[:, k, :],
                                     scaled[:, r % SCALED, :], start=False, stop=k == E // 2 - 1,
                                     skip_group_check=True).then_inc(S["moe_done"], 1)

        @block.gpsimd
        def _(pool):
            def zero(op, b):
                return nc.gpsimd.memset(op[ZERO_FROM:MAX_ROW, b, :, :].bitcast(U32), 0)

            zero(kop, 0).then_inc(S["zeroed_k"], 1)
            pool.wait_ge(S["zeroed_k"], 1)
            nc.gpsimd.memset(v_aug[:], 0.0).then_inc(S["pool_chain"], 1)
            pool.wait_ge(S["pool_chain"], 1)
            nc.gpsimd.memset(v_aug[:, :, :, :, DH:DH + 1], 1.0).then_inc(S["zeroed_v"], 1)
            pool.wait_ge(S["zeroed_v"], 1)
            zero(kop, 1).then_inc(S["zeroed_k"], 1)
            pool.wait_ge(S["zeroed_k"], 2)
            zero(qop, 1).then_inc(S["zeroed_q1"], 1)
            pool.wait_ge(S["zeroed_q1"], 1)
            chain = [1]

            def link(ins):
                chain[0] += 1
                ins.then_inc(S["pool_chain"], 1)
                pool.wait_ge(S["pool_chain"], chain[0])

            split_done = {}

            def split(first, parts, rest_, last_inc):
                link(nc.gpsimd.tensor_copy(parts[0], first))
                link(nc.gpsimd.tensor_tensor(rest_, first, parts[0], ALU.subtract))
                link(nc.gpsimd.tensor_copy(parts[1], rest_))
                nc.gpsimd.tensor_tensor(parts[2], rest_, parts[1], ALU.subtract).then_inc(S[last_inc], 1)
                split_done[last_inc] = split_done.get(last_inc, 0) + 1
                pool.wait_ge(S[last_inc], split_done[last_inc])

            for blk in range(len(BLOCKS)):
                pool.wait_ge(S["max_ready"], blk + 1)
                if blk >= 2:
                    pool.wait_ge(S["slot_free"], jobs_until("max_t", blk - 2))
                i = blk % 2
                split(negmax[:, i, :], [max_part[:, i, s, :] for s in range(3)], max_rest[:, i, :], "max_split")
                if blk == 0:
                    nc.gpsimd.memset(gate_part[:].bitcast(U32), 0).then_inc(S["gate_zeroed"], 1)
                    pool.wait_ge(S["gate_zeroed"], 1)
                if blk == 10:
                    pool.wait_ge(S["in_rest"], 16 * IN_REST)
                    split(expb_sb[:], [expb_part[:, s, :] for s in range(3)], expb_rest[:], "expb_split")

            for n, i in enumerate(BY_POOL):
                c, b, k = MOE[i]
                pool.wait_ge(S["gb_copied"], n + 1)
                if i >= SCALED:
                    pool.wait_ge(S["moe_done"], i - SCALED + 1)
                if n == 0:
                    pool.wait_ge(S["yt_ready"], 4)
                nc.gpsimd.tensor_tensor(scaled[:, i % SCALED, :], gate_copy[:, n % 2, :],
                                        yt2[:, b, c * NH:(c + 1) * NH], ALU.mult).then_inc(S["scaled_pool"], 1)
                pool.wait_ge(S["scaled_pool"], n + 1)

        @block.scalar
        def _(act):
            act.wait_ge(S["warm"], 1)
            nc.scalar.activation(warm[:, 1:2], warm[:, 0:1], ACT.Exp).then_inc(S["warm"], 1)
            act.wait_ge(S["in_qk"], 32)
            for b in range(B):
                for hf in range(HALVES):
                    act.wait_ge(S["qk_full"], HALVES * b + hf + 1)
                    nc.scalar.activation(part[0][:, b, hf * NH:(hf + 1) * NH], psum[:, 4 + HALVES * b + hf, :],
                                         ACT.Identity, bias=cols_sb[:, 0:1]).then_inc(S["part_h"], 1)
                for hf in range(HALVES):
                    act.wait_ge(S["part_r"], HALVES * b + hf + 1)
                    nc.scalar.activation(part[1][:, b, hf * NH:(hf + 1) * NH], rest[:, b, hf * NH:(hf + 1) * NH],
                                         ACT.Copy).then_inc(S["part_m"], 1)
            for u in range(UNITS + PV_LAG + 1):
                if u < UNITS:
                    if u >= P_RING:
                        act.wait_ge(S["pv_done"], u - P_RING + 1)
                    for pair in range(PAIRS):
                        s = PAIRS * u + pair
                        act.wait_ge(S["st_full"], s + 1)
                        nc.scalar.activation(probs[:, u % P_RING, 2 * pair:2 * pair + 2, :],
                                             psum[:, ST_BANKS[s % len(ST_BANKS)], :].rearrange("p (i n) -> p i n", i=2),
                                             ACT.Exp, scale=SCALE).then_inc(S["exp_done"], 1)
                w = u - PV_LAG - (TT - 1)
                if w >= 0 and w % TT == 0:
                    blk = w // TT
                    act.wait_ge(S["pv_done"], TT * (blk + 1))
                    if blk >= 2:
                        act.wait_ge(S["slot_free"], jobs_until("out_t", blk - 2))
                    nc.scalar.activation(o_sb[:, blk % 2, :], psum[:, PV_BANK, 0:QB], ACT.Copy).then_inc(S["o_copied"], 1)

            nc.scalar.activation(warm[:, 1:2], warm[:, 0:1], ACT.Sqrt).then_inc(S["warm"], 1)
            act.wait_ge(S["crw_full"], 1)
            nc.scalar.activation(cen_rw[:, P:], psum[:, 6, 0:B * E], ACT.Copy).then_inc(S["crw_ready"], 1)

            def roots(i, n):
                act.wait_ge(S["var_ready"], i + 1)
                nc.scalar.activation(root[:, 0:n], var_eps[:, 0:n], ACT.Sqrt).then_inc(S["root_ready"], 1)

            roots(0, 1)
            act.wait_ge(S["aff_ready"], 1)
            for c in range(2):
                nc.scalar.activation(aff[:, c * NH:(c + 1) * NH], psum[:, PROJ_BANKS[c], :], ACT.Identity,
                                     bias=shift[:], scale=gain[:]).then_inc(S["affine_done"], 1)
            for c in range(2):
                act.wait_ge(S["cen1_full"], c + 1)
                nc.scalar.activation(sq[:, 4 * c:4 * c + 4, :], psum[:, CEN_BANKS[c], :].rearrange("p (t c) -> p t c", t=4),
                                     ACT.Square).then_inc(S["sq1_ready"], 1)
            roots(1, TT * B)
            for c in range(2):
                act.wait_ge(S["zt_full"], c + 1)
                nc.scalar.activation(z_t[:, c * NH:(c + 1) * NH], psum[:, PROJ_BANKS[c], :], ACT.Copy).then_inc(S["zt_ready"], 1)
            for l in range(LAYERS):
                act.wait_ge(S["gv_full"], 2 * l + 1)
                nc.scalar.activation(gv[:, 0, :, :],
                                     psum[:, 7, 0:NHEAD * C // 2].rearrange("p (j c) -> p j c", c=C),
                                     ACT.Copy).then_inc(S["gv_act"], 1)
                act.wait_ge(S["tt_full"], l + 1)
                nc.scalar.activation(tt_l[:] if l < LAYERS - 1 else tt_f[:], psum[:, 7, 0:P],
                                     ACT.Copy).then_inc(S["tt_ready"], 1)
            for c in range(2):
                act.wait_ge(S["cen2_full"], c + 1)
                nc.scalar.activation(sq[:, 4 * c:4 * c + 4, :], cen2[:, 4 * c:4 * c + 4, 0:P],
                                     ACT.Square).then_inc(S["sq2_ready"], 1)
            roots(2, TT * B)

            nc.scalar.activation(warm[:, 1:2], warm[:, 0:1], ACT.Exp).then_inc(S["warm"], 1)
            act.wait_ge(S["logits_read"], 1)
            for t in range(TT):
                if t == TT - 2:
                    act.wait_ge(S["delta_ready"], 1)
                    nc.scalar.activation(ed[:], dlt[:], ACT.Exp).then_inc(S["exp2_ready"], 1)
                for b in range(B):
                    nc.scalar.activation(y[:, t, b, :, :],
                                         cen2[:, t:t + 1, b * C:(b + 1) * C].broadcast_to([P, 2, C]), ACT.Copy,
                                         scale=rstd[:, t * B + b:t * B + b + 1]).then_inc(S["y_ready"], 1)
            for i in range(4):
                c, b = divmod(i, 2)
                act.wait_ge(S["yt_full"], i + 1)
                nc.scalar.activation(yt2[:, b, c * NH:(c + 1) * NH], psum[:, YT_BANKS[i], :],
                                     ACT.Copy).then_inc(S["yt_ready"], 1)
            act.wait_ge(S["gt_full"], 1)
            nc.scalar.activation(gate_t[:, 0:NH], psum[:, GT_BANKS[0], 0:NH // 2].bitcast(BF16),
                                 ACT.Copy).then_inc(S["gt_ready"], 1)
            for n, i in enumerate(BY_POOL):
                act.wait_ge(S["gb_full"], i + 1)
                if n >= 2:
                    act.wait_ge(S["scaled_pool"], n - 1)
                nc.scalar.activation(gate_copy[:, n % 2, :], psum[:, GB_BANKS[i % len(GB_BANKS)], :],
                                     ACT.Copy).then_inc(S["gb_copied"], 1)

        @block.vector
        def _(dve):
            V = nc.vector
            chain = [0]

            def link(ins):
                chain[0] += 1
                ins.then_inc(S["dve_chain"], 1)
                dve.wait_ge(S["dve_chain"], chain[0])

            V.memset(warm[:], 0.0).then_inc(S["warm"], 1)
            V.memset(qop[ZERO_FROM:MAX_ROW, 0, :, :].bitcast(U32), 0).then_inc(S["zeroed_q"], 1)
            for b in range(B):
                for hf in range(HALVES):
                    at = slice(hf * NH, (hf + 1) * NH)
                    dve.wait_ge(S["part_h"], HALVES * b + hf + 1)
                    V.scalar_tensor_tensor(out=rest[:, b, at], in0=psum[:, 4 + HALVES * b + hf, :],
                                           scalar=cols_sb[:, 0:1], in1=part[0][:, b, at], op0=ALU.add,
                                           op1=ALU.subtract).then_inc(S["part_r"], 1)
                for hf in range(HALVES):
                    at = slice(hf * NH, (hf + 1) * NH)
                    dve.wait_ge(S["part_m"], HALVES * b + hf + 1)
                    V.tensor_tensor(part[2][:, b, at], rest[:, b, at], part[1][:, b, at],
                                    ALU.subtract).then_inc(S["part_l"], 1)
            dve.wait_ge(S["v_full"], 1)
            dve.wait_ge(S["zeroed_v"], 1)
            dve.wait_ge(S["in_v"], 32)
            for t in range(TT):
                last = V.tensor_tensor(v_aug[:, t, :, :, 0:DH].rearrange("p b h d -> p (b h) d"),
                                       psum[:, 2 + t // 4, (t % 4) * P:(t % 4 + 1) * P].rearrange("p (h d) -> p h d", d=DH),
                                       bv_sb[:].rearrange("p (h d) -> p h d", d=DH), ALU.add)
            last.then_inc(S["v_ready"], 1)

            for r, (kind, blk, k, c) in enumerate(SLOT_JOBS):
                bank = slot_bank[r]
                b, g, qb = BLOCKS[blk]
                i = blk % 2
                dve.wait_ge(S["slot_full"], r + 1)
                if kind == "max":
                    if k == 0 and c == 0 and blk >= 2:
                        dve.wait_ge(S["max_split"], blk - 1)
                    V.tensor_reduce(negmax_half[:, i, c, k:k + 1], psum[:, bank, :], AX_X, ALU.max,
                                    negate=True).then_inc(S["slot_free"], 1)
                    if k == TT - 1 and c == HALVES - 1:
                        dve.wait_ge(S["slot_free"], r + 1)
                        V.tensor_tensor(negmax[:, i, :], negmax_half[:, i, 0, :], negmax_half[:, i, 1, :],
                                        ALU.min).then_inc(S["max_ready"], 1)
                elif kind == "max_t":
                    if blk >= 2:
                        dve.wait_ge(mrow_in[i], 16 * (blk // 2))
                    V.tensor_copy(max_row[:, i, :], psum[0:3 * HG * QT, bank, 0:P // 2].bitcast(BF16)
                                  ).then_inc(S["slot_free"], 1)
                elif kind == "attn_t":
                    V.tensor_copy(attn_t[:, blk * NH:(blk + 1) * NH], psum[:, bank, :]).then_inc(S["slot_free"], 1)
                    dve.wait_ge(S["proj_full"], blk + 1)
                    link(V.bn_stats(bn[:, blk, :], psum[:, PROJ_BANKS[blk], :]))
                else:
                    o = psum[:, bank, 0:QT * P].rearrange("p (t j v) -> p t j v", t=QT, j=HG)
                    link(V.reciprocal(rden[:, i, :, :], o[:, :, :, DH]))
                    dst = attn[:, qb * QT:(qb + 1) * QT, b, g * HG * DH:(g + 1) * HG * DH]
                    V.tensor_tensor(dst.rearrange("p t (j d) -> p t j d", j=HG), o[:, :, :, 0:DH],
                                    rden[:, i, :, :].rearrange("p t (j o) -> p t j o", o=1).broadcast_to([P, QT, HG, DH]),
                                    ALU.mult).then_inc(S["slot_free"], 1)

            link(V.bn_aggr(mv[:], bn[:].rearrange("p a b -> p (a b)")))
            V.tensor_tensor(mean_b[:], mv[:, 0:1], cols_sb[:, 1:2], ALU.add).then_inc(S["mean_ready"], 1)
            dve.wait_ge(S["mean_full"], 1)
            dve.wait_ge(S["mean_ready"], 1)
            link(V.tensor_tensor(diff[:], psum[:, 4, 0:1], mean_b[:], ALU.add))
            V.scalar_tensor_tensor(out=dev[:], in0=diff[:], scalar=diff[:], in1=mv[:, 1:2], op0=ALU.mult,
                                   op1=ALU.add).then_inc(S["dev_ready"], 1)
            link(V.tensor_tensor(neg_mean[:], psum[:, 4, 0:1], cols_sb[:, 1:2], ALU.add))

            def reciprocal_root(i, variance, scale, out, n):
                v, y0, w = var_eps[:, 0:n], root[:, 0:n], newton[:, 0:n]
                V.tensor_scalar(v, variance, scale, EPS, ALU.mult, ALU.add).then_inc(S["var_ready"], 1)
                dve.wait_ge(S["var_ready"], i + 1)
                dve.wait_ge(S["root_ready"], i + 1)
                link(V.reciprocal(y0, y0))
                link(V.tensor_tensor(w, y0, y0, ALU.mult))
                link(V.scalar_tensor_tensor(out=w, in0=w, scalar=-0.5, in1=v, op0=ALU.mult, op1=ALU.mult))
                return V.scalar_tensor_tensor(out=out, in0=w, scalar=1.5, in1=y0, op0=ALU.add, op1=ALU.mult)

            dve.wait_ge(S["var_full"], 1)
            link(reciprocal_root(0, psum[:, 5, 0:1], 1.0, grstd[:], 1))
            link(V.tensor_tensor(gain[:], grstd[:], cols_sb[:, 2:3], ALU.mult))
            V.scalar_tensor_tensor(out=shift[:], in0=neg_mean[:], scalar=gain[:], in1=cols_sb[:, 3:4], op0=ALU.mult,
                                   op1=ALU.add).then_inc(S["aff_ready"], 1)
            for c in range(2):
                dve.wait_ge(S["affine_done"], c + 1)
                V.tensor_tensor(t1[:, c * NH:(c + 1) * NH], aff[:, c * NH:(c + 1) * NH], x_sb[:, c * NH:(c + 1) * NH],
                                ALU.add).then_inc(S["t1_ready"], 1)

            def token_rstd(norm):
                for c in range(2):
                    dve.wait_ge(S[f"sq{norm}_ready"], c + 1)
                    last = V.tensor_reduce(ssq[:, 8 * c:8 * c + 8],
                                           sq[:, 4 * c:4 * c + 4, :].rearrange("p t (b c) -> p (t b) c", b=B), AX_X,
                                           ALU.add)
                link(last)
                return reciprocal_root(norm, ssq[:], 1.0 / C, rstd[:], TT * B)

            link(token_rstd(1))
            for c in range(2):
                V.tensor_tensor(z[:, 4 * c:4 * c + 4, :].rearrange("p t (b c) -> p t b c", b=B),
                                psum[:, CEN_BANKS[c], :].rearrange("p (t b c) -> p t b c", b=B, c=C),
                                rstd[:, 8 * c:8 * c + 8].rearrange("p (t b o) -> p t b o", b=B, o=1)
                                .broadcast_to([P, 4, B, C]), ALU.mult).then_inc(S["z_ready"], 1)
            dve.wait_ge(S["gram0_full"], 1)
            V.tensor_tensor(gram[:], psum[:, 6, 0:P], diag_mask, ALU.mult).then_inc(S["gram_ready"], 1)
            for l in range(LAYERS):
                dve.wait_ge(S["gv_full"], 2 * l + 2)
                V.tensor_copy(gv[:, 1, :, :],
                              psum[:, 5, 0:NHEAD * C // 2].rearrange("p (j c) -> p j c", c=C)).then_inc(S["gv_dve"], 1)
                dve.wait_ge(S["m_full"], l + 1)
                V.scalar_tensor_tensor(out=w_l[:].rearrange("p (b c) -> p b c", b=B),
                                       in0=psum[:, 4:5, 0:C].broadcast_to([P, B, C]), scalar=1.0 / (N * NHEAD),
                                       in1=diag_mask.rearrange("p (b c) -> p b c", b=B),
                                       op0=ALU.mult, op1=ALU.mult).then_inc(S["w_ready"], 1)
                if l < LAYERS - 1:
                    dve.wait_ge(S["u_full"], l + 1)
                    V.tensor_copy(u_l[:], psum[:, 6, 0:P]).then_inc(S["u_ready"], 1)
                    dve.wait_ge(S["gram_full"], l + 1)
                    V.tensor_copy(gram[:], psum[:, 5, 0:P]).then_inc(S["gram_ready"], 1)
            for c in range(2):
                dve.wait_ge(S["attn2_full"], c + 1)
                V.tensor_tensor(t2[:, c * NH:(c + 1) * NH], psum[:, c, :], t1[:, c * NH:(c + 1) * NH],
                                ALU.add).then_inc(S["t2_ready"], 1)
            token_rstd(2).then_inc(S["rstd_ready"], 1)
            dve.wait_ge(S["rstd_ready"], 1)

            G8 = TT * B // 2

            def halves(step):
                for c in range(2):
                    dve.wait_ge(S["dve_chain"], chain[0] - 1)
                    chain[0] += 1
                    step(c).then_inc(S["dve_chain"], 1)

            def of(v, c):
                return v[:, c * G8:(c + 1) * G8]

            def over_e(v, c):
                return of(v, c).rearrange("p (a o) -> p a o", o=1).broadcast_to([P, G8, E])

            def over_tokens(v):
                return v[:].rearrange("p (o e) -> p o e", o=1).broadcast_to([P, G8, E])

            dve.wait_ge(S["in_rest"], 16 * IN_REST)
            V.tensor_tensor(lg[:].rearrange("p (t b) e -> p t b e", b=B),
                            cen2[:, :, P:P + B * E].rearrange("p t (b e) -> p t b e", b=B),
                            rstd[:].rearrange("p (t b o) -> p t b o", b=B, o=1).broadcast_to([P, TT, B, E]),
                            ALU.mult).then_inc(S["logits_read"], 1)
            dve.wait_ge(S["logits_read"], 1)
            halves(lambda c: V.tensor_tensor(of(lg, c), of(lg, c), over_tokens(rb_sb), ALU.add))

            def one_hot_of_largest(logits, largest, hot):
                halves(lambda c: V.tensor_reduce(of(largest, c), of(logits, c), AX_X, ALU.max))
                halves(lambda c: V.tensor_tensor(of(cand, c), of(logits, c), over_e(largest, c), ALU.is_equal))
                halves(lambda c: V.tensor_tensor(of(cand, c), of(cand, c), over_tokens(weight_sb), ALU.mult))
                halves(lambda c: V.tensor_reduce(of(pick, c), of(cand, c), AX_X, ALU.max))
                halves(lambda c: V.tensor_tensor(of(hot, c), over_tokens(weight_sb), over_e(pick, c), ALU.is_equal))

            one_hot_of_largest(lg, m1, hot1)
            halves(lambda c: V.scalar_tensor_tensor(out=of(lg2, c), in0=of(hot1, c), scalar=-3e38, in1=of(lg, c),
                                                    op0=ALU.mult, op1=ALU.add))
            one_hot_of_largest(lg2, m2, hot2)
            V.tensor_tensor(dlt[:], m2[:], m1[:], ALU.subtract).then_inc(S["delta_ready"], 1)
            dve.wait_ge(S["exp2_ready"], 1)
            link(V.tensor_scalar(gate1[:], ed[:], 1.0, None, ALU.add))
            halves(lambda c: V.tensor_tensor(of(hot2, c), of(hot2, c), over_e(ed, c), ALU.mult))
            link(V.reciprocal(gate1[:], gate1[:]))
            halves(lambda c: V.tensor_tensor(of(gates, c), of(hot1, c), of(hot2, c), ALU.add))
            halves(lambda c: V.tensor_tensor(of(gates, c), of(gates, c), over_e(gate1, c), ALU.mult))
            dve.wait_ge(S["gate_zeroed"], 1)

            def by_tile(v, c):
                return of(v, c).rearrange("p (t b) e -> p t (b e)", b=B)

            def gp(s, c):
                return gate_part[:, c * TT // 2:(c + 1) * TT // 2, s * B * E:(s + 1) * B * E]

            halves(lambda c: V.tensor_copy(gp(0, c), by_tile(gates, c)))
            halves(lambda c: V.tensor_tensor(by_tile(gate_rest, c), by_tile(gates, c), gp(0, c), ALU.subtract))
            halves(lambda c: V.tensor_copy(gp(1, c), by_tile(gate_rest, c)))
            for c in range(2):
                dve.wait_ge(S["dve_chain"], chain[0] - 1 + c)
                V.tensor_tensor(gp(2, c), by_tile(gate_rest, c), gp(1, c), ALU.subtract).then_inc(S["gate_split"], 1)
            dve.wait_ge(S["gt_full"], 2)
            V.tensor_copy(gate_t[:, NH:], psum[:, GT_BANKS[1], 0:NH // 2].bitcast(BF16)).then_inc(S["gt_ready2"], 1)
            for n, i in enumerate(BY_DVE):
                c, b, k = MOE[i]
                dve.wait_ge(S["gb_full"], i + 1)
                if i >= SCALED:
                    dve.wait_ge(S["moe_done"], i - SCALED + 1)
                V.tensor_tensor(scaled[:, i % SCALED, :], psum[:, GB_BANKS[i % len(GB_BANKS)], :],
                                yt2[:, b, c * NH:(c + 1) * NH], ALU.mult).then_inc(S["scaled_dve"], 1)
                if i == BY_DVE[-3]:
                    dve.wait_ge(S["moe_done"], len(MOE) // 2)
                    V.tensor_tensor(res[:, 0:NH], psum[:, MOE_BANKS[0], :], t2[:, 0:NH], ALU.add).then_inc(S["out_done"], 1)
            dve.wait_ge(S["moe_done"], len(MOE))
            V.tensor_tensor(res[:, NH:], psum[:, MOE_BANKS[1], :], t2[:, NH:], ALU.add).then_inc(S["out_done"], 1)


def kernel(**inputs):
    import numpy as np
    import concourse.bacc as bacc
    from concourse.bass_utils import run_bass_kernel_spmd

    f32 = np.float32
    get = {k.removeprefix("L0_conv_").removeprefix("L1_"): np.asarray(v, f32) for k, v in inputs.items()}

    def diag(a, n=B):
        out = np.zeros((n * a.shape[0], n * a.shape[1]), a.dtype)
        for i in range(n):
            out[i * a.shape[0]:(i + 1) * a.shape[0], i * a.shape[1]:(i + 1) * a.shape[1]] = a
        return out

    x = get["x"].reshape(P, N)

    def by_channel(q, k):
        return np.stack([q, k]).reshape(2, H, DH, -1).transpose(2, 0, 1, 3).reshape(P, -1)

    qk = by_channel(get["Wq"], get["Wk"]).T
    wqk = np.zeros((P, B, P), f32)
    for b in range(B):
        wqk[b * C:(b + 1) * C, b] = qk
    cols = np.stack([by_channel(get["bq"], get["bk"])[:, 0]] + [np.tile(get[n], B) for n in ("bo", "gn_w", "gn_b")], 1)
    bv_row = np.broadcast_to(np.tile(get["bv"], B), (P, P))
    v, q = get["attn_v_matrix"][:, :, 0], get["attn_q_matrix"][:, :, 0]
    by_parity = v.reshape(LAYERS, NHEAD // 2, 2, C, C)
    vt = np.tile(by_parity.transpose(4, 0, 2, 1, 3).reshape(C, LAYERS, 2, NHEAD // 2 * C), (B, 1, 1, 1))
    q_pairs = q.reshape(LAYERS, NHEAD // 2, 2, C, C).transpose(2, 4, 0, 1, 3).reshape(P, LAYERS, NHEAD // 2, C)
    cen_r = diag(get["ffn_router_w"])
    expw = get["ffn_expert_w"].reshape(E // 2, 2 * C, C).transpose(1, 0, 2)
    expb = np.zeros((P, P), f32)
    expb[:3 * B * E] = np.tile(diag(get["ffn_expert_b"]), (3, 1))
    rb_row = np.broadcast_to(get["ffn_router_b"], (P, E))

    eye = np.eye(P, dtype=f32)
    group = C // 8
    avg = np.kron(np.eye(P // group), np.full((group, group), 1.0 / group)).astype(f32)
    centre = eye - diag(np.full((C, C), 1.0 / C, f32))
    consts = np.concatenate([eye, centre, -avg, avg, diag(np.ones((C, C), f32)), eye * (N * NHEAD),
                             np.broadcast_to(np.arange(E, 0, -1, dtype=f32), (P, E)), np.tile(np.eye(C, dtype=f32), (B, 1))], 1)
    select = np.zeros((P, B * E // 2, P), f32)
    for s in range(3):
        for b in range(B):
            for e in range(E):
                select[(s * B + b) * E + e, b * (E // 2) + e // 2, (e % 2) * C:(e % 2 + 1) * C] = 1
    import ml_dtypes
    bf = ml_dtypes.bfloat16
    cbf = np.concatenate([eye.astype(bf), select.reshape(P, -1).astype(bf)], 1)
    ones = np.ones((3, B, H, N), bf)

    nc = bacc.Bacc("TRN2", target_bir_lowering=False, num_devices=1)
    arrays, args = {}, []
    for name, a in dict(x=x, wqk=wqk, wv=diag(get["Wv"].T.copy()), wo=diag(get["Wo"].T.copy()), cols=cols, bv_row=bv_row, vt=vt,
                        q_pairs=q_pairs, router=cen_r, expw=expw, expb=expb, rb_row=rb_row, consts=consts, cbf=cbf,
                        ones=ones).items():
        a = np.ascontiguousarray(a)
        arrays[f"in_{name}"] = a
        args.append(nc.dram_tensor(f"in_{name}", a.shape, mybir.dt.from_np(a.dtype), kind="ExternalInput").ap())
    args.append(nc.dram_tensor("out", (P, N), F32, kind="ExternalOutput").ap())
    conv_attn_hybrid_kernel(nc, *args)
    r = run_bass_kernel_spmd(nc, [arrays], core_ids=[0])
    return r.results[0]["out"].reshape(B, C, 32, 32)
```

```python
from contextlib import ExitStack

from concourse import mybir

ALU = mybir.AluOpType
ACT = mybir.ActivationFunctionType
AX_X = mybir.AxisListType.X
F32 = mybir.dt.float32
BF16 = mybir.dt.bfloat16
U32 = mybir.dt.uint32

P = 128
B = 2
C = 64
N = 1024
H = 8
DH = C // H
HG = 4
NG = H // HG
NH = 512
HALVES = N // NH
TT = N // P
QB = 256
QT = QB // P
BLOCKS = [(b, g, qb) for b in range(B) for g in range(NG) for qb in range(N // QB)]
UNITS = TT * len(BLOCKS)
PAIRS = HG // 2
VW = 32
LAYERS = 4
NHEAD = 8
E = 8
SCALE = float(DH) ** -0.5
EPS = 1e-5

PARTS = 3
STORED = PARTS + 2
PART_ROWS = DH * PARTS
ZERO_FROM = 64
MAX_ROW = 96
SCORE_ROWS = MAX_ROW + 3

WARM_COLS = 256
SELECTED = [("q", 0, 0), ("k", 0, 0), ("k", 0, 1), ("k", 1, 0), ("k", 1, 1),
            ("q", 1, 0), ("k", 2, 0), ("k", 2, 1), ("k", 3, 0), ("k", 3, 1)]
SELECT_BEFORE = [0, 0, 0, 1, 1, 2, 2, 3, 4, 5]
SELECTED_NEED = [3, 3, 5, 5, 8, 8, 10, 10]
SEL_BANKS = (4, 5, 1, 4, 5, 4, 5, 4, 5, 4)
LEAD = 11
CATCH_UP = (1, 3, 5, 7)
DIRECT = 2
PV_LAG = 3
ST_BANKS = (4, 5, 6)
PV_BANK = 7
P_RING = 8
IN_REST = 10
PROJ_BANKS = (1, 3)
CEN_BANKS = (0, 2, 4, 5)
QUARTER = N // P // 4
LN1_ORDER = (2, 3, 0, 1)
PIECES = ((0, 4), (4, 6), (6, 8))
YT_BANKS = (6, 7, 0, 1)
GT_BANKS = (2, 5)
GB_BANKS = (3, 4, 0, 1, 5)
MOE_BANKS = (6, 7)
OUT_PIECES = ((0, NH), (NH, NH + QB), (NH + QB, N))
GB_LAG = 4
MOE = [(c, b, k) for c in range(2) for k in range(E // 2) for b in range(B)]
BY_POOL = [i for i in range(len(MOE)) if i % 3 == 1]
BY_DVE = [i for i in range(len(MOE)) if i not in BY_POOL]
SCALED = 6


def conv_attn_hybrid_kernel(nc, x, wqk, sel, wv, wo, cols, bv_row, vt, q_pairs, router, expw, expb, rb_row, consts, cbf, ones, out):
    with ExitStack() as ctx:
        def sb(name, shape, dt=F32):
            return ctx.enter_context(nc.sbuf_tensor(name, shape, dt))

        def sem(name):
            return ctx.enter_context(nc.semaphore(name))

        parts_dram = nc.dram_tensor("parts_scratch", (B, STORED, P, N), BF16, kind="Internal").ap()
        max_dram = nc.dram_tensor("max_scratch", (len(BLOCKS), 3 * HG * QT, P), BF16, kind="Internal").ap()
        psum = ctx.enter_context(nc.psum_tensor("psum", [P, 8, 512], F32))

        cen2 = psum[:, 2:6, :].rearrange("p a (h n) -> p (a h) n", h=2)

        x_sb = sb("x_sb", [P, N])
        wqk_sb = sb("wqk_sb", [P, B, P])
        wv_sb = sb("wv_sb", [P, P])
        sel_sb = sb("sel_sb", [P, 2, HG, PARTS, MAX_ROW], BF16)
        idle = sb("idle", [P, P], BF16)
        wo_sb = sb("wo_sb", [P, P])
        cols_sb = sb("cols_sb", [P, 4])
        bv_sb = sb("bv_sb", [P, P])
        vt_sb = sb("vt_sb", [P, LAYERS, 2, NHEAD // 2 * C])
        q_pair = sb("q_pair", [P, LAYERS, NHEAD // 2, C])
        rw_sb = sb("rw_sb", [P, B * E])
        expw_sb = sb("expw_sb", [P, E // 2, C])
        expb_sb = sb("expb_sb", [P, P])
        rb_sb = sb("rb_sb", [P, E])
        consts_sb = sb("consts_sb", [P, 6, P])
        eye2_sb = sb("eye2_sb", [P, C])
        ident, centre, neg_avg, avg, diag_mask, ident_n = (consts_sb[:, i, :] for i in range(6))
        weight_sb = sb("weight_sb", [P, E])
        cbf_sb = sb("cbf_sb", [P, 1 + B * E // 2, P], BF16)
        ident_bf = cbf_sb[:, 0, :]
        select = cbf_sb[:, 1:, :]

        part = [sb(f"part{i}", [P, B, N], BF16) for i in range(3)]
        rest = sb("rest", [P, B, N])
        warm = sb("warm", [P, 2])
        qop = sb("qop", [P, B, H, N], BF16)
        kop = sb("kop", [P, B, H, N], BF16)
        v_aug = sb("v_aug", [P, TT, B, H, VW])
        negmax_half = sb("negmax_half", [P, 2, HALVES, HG * QT])
        negmax = sb("negmax", [P, 2, HG * QT])
        max_rest = sb("max_rest", [P, 2, HG * QT])
        max_part = sb("max_part", [P, 2, 3, HG * QT], BF16)
        max_row = sb("max_row", [3 * HG * QT, 2, P], BF16)
        probs = sb("probs", [P, P_RING, HG, QB])
        o_sb = sb("o_sb", [P, 2, QB])
        rden = sb("rden", [P, 2, QT, HG])
        attn = sb("attn", [P, TT, B, C])

        spare_q = qop[:].rearrange("p b h n -> p (b h n)").bitcast(F32)
        y = spare_q[:, 0:2 * N].rearrange("p (t b u c) -> p t b u c", t=TT, b=B, u=2)
        yt2 = spare_q[:, 2 * N:4 * N].rearrange("p (b n) -> p b n", b=B)
        res = spare_q[:, 4 * N:5 * N]
        scaled = spare_q[:, 5 * N:5 * N + SCALED * NH].rearrange("p (i n) -> p i n", n=NH)
        spare = probs[:].rearrange("p u j n -> p (u j n)").rearrange("p (a n) -> p a n", n=N)
        aff, t1, z_t, t2 = (spare[:, i, :] for i in range(4))
        gate_copy = spare[:, 4, :].rearrange("p (i n) -> p i n", n=NH)
        z, sq = (spare[:, i, :].rearrange("p (t c) -> p t c", c=P) for i in (6, 7))
        attn_t = sb("attn_t", [P, N])
        bn = sb("bn", [P, N // QB, 6])
        mv = sb("mv", [P, 2])
        neg_mean, mean_b, diff, dev, grstd, gain, shift = (sb(n, [P, 1]) for n in ("neg_mean", "mean_b", "diff", "dev", "grstd", "gain", "shift"))
        ssq = sb("ssq", [P, TT * B])
        rstd = sb("rstd", [P, TT * B])
        var_eps = sb("var_eps", [P, TT * B])
        root = sb("root", [P, TT * B])
        newton = sb("newton", [P, TT * B])
        gram = sb("gram", [P, P])
        gv = sb("gv", [P, B, NHEAD // 2, C])
        w_l = sb("w_l", [P, P])
        u_l = sb("u_l", [P, P])
        tt_l = sb("tt_l", [P, P])
        tt_f = sb("tt_f", [P, P])
        cen_rw = sb("cen_rw", [P, P + B * E])
        lg = sb("lg", [P, TT * B, E])
        lg2 = sb("lg2", [P, TT * B, E])
        m1 = sb("m1", [P, TT * B])
        m2 = sb("m2", [P, TT * B])
        cand = sb("cand", [P, TT * B, E])
        pick = sb("pick", [P, TT * B])
        hot1 = sb("hot1", [P, TT * B, E])
        hot2 = sb("hot2", [P, TT * B, E])
        dlt = sb("dlt", [P, TT * B])
        ed = sb("ed", [P, TT * B])
        gate1 = sb("gate1", [P, TT * B])
        gates = sb("gates", [P, TT * B, E])
        gate_rest = sb("gate_rest", [P, TT * B, E])
        gate_part = sb("gate_part", [P, TT, P], BF16)
        gate_t = sb("gate_t", [P, N], BF16)
        expb_part = sb("expb_part", [P, 3, P], BF16)
        expb_rest = sb("expb_rest", [P, P])

        names = (
            "warm in_x in_qk in_c in_v in_sel in_bv idle_ready rows0_full rows0_in sel_full sel_act sel_dve v_out parts1_in parts1 in_ident in_rest zeroed_q zeroed_q1 zeroed_k zeroed_v v_ready qk_full part_h part_r part_m part_l v_full "
            "slot_full slot_free st_full exp_done pv_done o_copied out_written pool_chain max_ready max_split max_out "
            "dve_chain proj_full crw_full crw_ready mean_ready mean_full dev_ready var_full "
            "aff_ready affine_done t1_ready cen1_full sq1_ready z_ready gram0_full zt_full zt_ready gv_full gv_act gv_dve "
            "m_full w_ready u_full u_ready tt_full tt_ready gram_full gram_ready attn2_full t2_ready cen2_full sq2_ready "
            "y_ready yt_full yt_ready logits_read delta_ready exp2_ready gate_zeroed gate_split gt_full "
            "gt0_ready var_ready root_ready rstd_ready gt1_ready gb_full gb_copied scaled_dve scaled_pool moe_done out_done expb_split").split()
        S = {n: sem(n) for n in names}
        ops_ready = [[sem(f"ops_ready{b}{g}") for g in range(NG)] for b in range(B)]
        mrow_in = [sem(f"mrow_in{i}") for i in range(2)]
        N_OPS = [[PARTS, 2 * PARTS], [2 * PARTS, 2 * PARTS]]
        parts_out = [sem(f"parts_out{b}") for b in range(B)]

        jobs_at = {}
        EARLY = TT * (len(BLOCKS) - 2) + PV_LAG + 3
        for u in range(-LEAD, UNITS + 8):
            jobs = []
            for v in range(u + LEAD + sum(e < u for e in CATCH_UP), u + LEAD + 1 + sum(e <= u for e in CATCH_UP)):
                if 0 <= v < UNITS:
                    blk, k = divmod(v, TT)
                    jobs += [("max", blk, k, c) for c in range(HALVES)]
                if v >= 2 * TT + 2 and (v - 2) % TT == 0 and (v - 2) // TT <= len(BLOCKS):
                    blk = (v - 2) // TT - 1
                    jobs += [("max_r", blk, 0, c) for c in range(HALVES)] if blk < DIRECT else [("max_t", blk, 0, 0)]
            w = u - PV_LAG - 1
            if w >= TT and w % TT == 0 and w // TT <= len(BLOCKS):
                jobs.append(("out_t", w // TT - 1, 0, 0))
            if u == EARLY:
                jobs.append(("attn_t", 0, 0, 0))
            if u == UNITS + PV_LAG + 2:
                jobs.append(("attn_t", 2, 0, 0))
            if u == UNITS - TT + PV_LAG + 2:
                jobs.append(("attn_t", 1, 0, 0))
            jobs_at[u] = sorted(jobs, key=lambda job: job[0] != "max")
        SLOT_JOBS = [j for u in range(-LEAD, UNITS + 8) for j in jobs_at[u]]

        LAST_MAX = max(r for r, job in enumerate(SLOT_JOBS) if job[0] == "max")
        slot_bank = [r % 4 if r <= LAST_MAX else 2 * (r % 2) for r in range(len(SLOT_JOBS))]

        def bank_free_at(r):
            return max([p for p in range(r) if slot_bank[p] == slot_bank[r]], default=-1) + 1

        def jobs_until(kind, blk):
            return max(r for r, job in enumerate(SLOT_JOBS) if job[:2] == (kind, blk)) + 1

        block = ctx.enter_context(nc.Block())

        @block.sync
        def _(sp):
            sp.dma_start(x_sb[:], x).then_inc(S["in_x"], 16)
            sp.dma_start(cols_sb[:], cols).then_inc(S["in_qk"], 16)
            sp.dma_start(wqk_sb[:], wqk).then_inc(S["in_qk"], 16)
            sp.dma_start(wv_sb[:], wv).then_inc(S["in_v"], 16)
            sp.dma_start(sel_sb[:], sel).then_inc(S["in_sel"], 16)
            sp.dma_start(bv_sb[:], bv_row).then_inc(S["in_bv"], 16)
            sp.dma_start(cbf_sb[:], cbf.rearrange("p (a n) -> p a n", n=P)).then_inc(S["in_c"], 16)
            sp.dma_start(kop[MAX_ROW:SCORE_ROWS, :, :, :], ones).then_inc(S["in_c"], 16)
            sp.wait_ge(S["zeroed_q"], 1)
            sp.wait_ge(S["zeroed_k"], 1)
            def store_parts(b):
                for i, name in enumerate(("part_h", "part_m", "part_l")):
                    sp.wait_ge(S["parts1" if b else name], HALVES)
                    for stored in range(i, STORED, PARTS):
                        sp.dma_start(parts_dram[b, stored, :, :], part[i][:, b, :]).then_inc(parts_out[b], 16)

            def operands(b, g):
                sp.wait_ge(parts_out[b], 16 * STORED)
                sp.wait_ge(S["zeroed_k"], b + 1)
                sp.wait_ge(S["zeroed_q1" if b else "zeroed_q"], 1)
                first = b == 0 and g == 0
                at = QB if first else 0
                rows = parts_dram[b].rearrange("s (d w h) n -> (s d) w h n", d=DH, w=2)
                heads = slice(g * HG, (g + 1) * HG)
                for r in range(PARTS):
                    to = slice(r * PART_ROWS, (r + 1) * PART_ROWS)
                    sp.dma_start(qop[to, b, heads, at:], rows[0:PART_ROWS, 0, heads, at:]).then_inc(ops_ready[b][g], 16)
                    if not first:
                        sp.dma_start(kop[to, b, heads, :],
                                     rows[r * DH:r * DH + PART_ROWS, 1, heads, :]).then_inc(ops_ready[b][g], 16)

            def max_rows(i):
                b, g, qb = BLOCKS[i]
                sp.wait_ge(S["slot_free"], jobs_until("max_t", i))
                sp.dma_start(max_dram[i], max_row[:, i % 2, :]).then_inc(S["max_out"], 16)
                sp.wait_ge(S["max_out"], 16 * (i - DIRECT + 1))
                sp.dma_start(qop[MAX_ROW:SCORE_ROWS, b, g * HG:(g + 1) * HG, qb * QB:(qb + 1) * QB],
                             max_dram[i].rearrange("(s j t) n -> s j (t n)", s=PARTS, j=HG)).then_inc(mrow_in[i % 2], 16)

            store_parts(0)
            operands(0, 0)
            operands(0, 1)
            sp.dma_start(consts_sb[:], consts[:, 0:6 * P].rearrange("p (a n) -> p a n", n=P)).then_inc(S["in_ident"], 16)
            max_rows(2)
            store_parts(1)
            operands(1, 0)
            max_rows(3)
            operands(1, 1)
            max_rows(4)
            for at, source in ((weight_sb[:], consts[:, 6 * P:6 * P + E]), (cen_rw[:, 0:P], consts[:, P:2 * P]),
                               (rw_sb[:], router), (wo_sb[:], wo), (expw_sb[:], expw), (expb_sb[:], expb),
                               (rb_sb[:], rb_row),
                               (eye2_sb[:], consts[:, 6 * P + E:])):
                sp.dma_start(at, source).then_inc(S["in_rest"], 16)
            max_rows(5)
            sp.dma_start(vt_sb[:], vt).then_inc(S["in_rest"], 16)
            sp.dma_start(q_pair[:], q_pairs).then_inc(S["in_rest"], 16)
            for i in range(6, len(BLOCKS)):
                max_rows(i)
            for n, (first, end) in enumerate(OUT_PIECES):
                sp.wait_ge(S["out_done"], n + 1)
                sp.dma_start(out[:, first:end], res[:, first:end]).then_inc(S["out_written"], 16)
            sp.wait_ge(S["out_written"], 16 * len(OUT_PIECES))

        @block.tensor
        def _(pe):
            pe.wait_ge(S["idle_ready"], 1)
            for _ in range(30):
                nc.tensor.matmul(psum[:, SEL_BANKS[0], 0:P], idle[:, 0:P], idle[:],
                                 start=True, stop=True, skip_group_check=True)
            pe.wait_ge(S["in_x"], 16)
            pe.wait_ge(S["in_qk"], 32)

            def queries_and_keys(b):
                for hf in range(HALVES):
                    nc.tensor.matmul(psum[:, 4 + HALVES * b + hf, :], wqk_sb[:, b, :], x_sb[:, hf * NH:(hf + 1) * NH],
                                     start=True, stop=True).then_inc(S["qk_full"], 1)

            queries_and_keys(0)
            pe.wait_ge(S["in_v"], 16)
            for t in range(TT):
                last = nc.tensor.matmul(psum[:, 2 + t // 4, (t % 4) * P:(t % 4 + 1) * P], x_sb[:, t * P:(t + 1) * P],
                                        wv_sb[:], start=True, stop=True, skip_group_check=True)
                if t % 4 == 3:
                    last.then_inc(S["v_full"], 1)

            def select_operand(i):
                what, a, hf = SELECTED[i]
                if i < 2:
                    pe.wait_ge(S["part_r"], i + 1)
                elif i == 4:
                    pe.wait_ge(S["sel_dve"], 1)
                elif i > 2:
                    pe.wait_ge(S["sel_act"], i - 2 if i > 4 else 1)
                heads = (2 * a, 2 * a + 1) if what == "q" else (a,)
                for n, h in enumerate(heads):
                    at = slice(0, QB) if what == "q" else slice(hf * NH, (hf + 1) * NH)
                    for s, name in enumerate(("part_h", "part_m", "part_l")):
                        if i < 3:
                            pe.wait_ge(S[name], hf + 1)
                        size = at.stop - at.start
                        last = nc.tensor.matmul(psum[0:MAX_ROW, SEL_BANKS[i], n * size:(n + 1) * size],
                                                sel_sb[:, int(what == "k"), h, s, :], part[s][:, 0, at],
                                                start=s == 0, stop=s == PARTS - 1, skip_group_check=True)
                last.then_inc(S["sel_full"], 1)

            def rows_of_max(blk, c, bank):
                pe.wait_ge(S["max_split"], blk + 1)
                pe.wait_ge(S["in_c"], 32)
                for n in range(PAIRS * QT):
                    last = nc.tensor.matmul(psum[MAX_ROW:SCORE_ROWS, bank, n * P:(n + 1) * P],
                                            max_part[:, blk % 2, :, c * PAIRS * QT + n], ident_bf,
                                            start=True, stop=True, skip_group_check=True)
                return last

            slot = [0]

            def fill_slot(job):
                kind, blk, k, c = job
                r = slot[0]
                slot[0] += 1
                bank = slot_bank[r]
                if bank_free_at(r):
                    pe.wait_ge(S["slot_free"], bank_free_at(r))
                b, g, qb = BLOCKS[blk]
                if kind == "max":
                    if blk == 0 and c == 0:
                        if k == 0:
                            pe.wait_ge(S["in_sel"], 16)
                        for i in range(len(SELECTED)):
                            if SELECT_BEFORE[i] == k:
                                select_operand(i)
                        pe.wait_ge(S["sel_dve"], 1)
                        pe.wait_ge(S["sel_act"], SELECTED_NEED[k] - 2)
                    elif blk == 0:
                        pe.wait_ge(S["sel_act"], SELECTED_NEED[k] - 1)
                    elif k == 0 and c == 0:
                        if blk == 1:
                            queries_and_keys(1)
                        pe.wait_ge(ops_ready[b][g], 16 * N_OPS[b][g])
                    if r == 2:
                        pe.wait_ge(S["v_out"], 2)
                    j, t = divmod(k, QT)
                    last = nc.tensor.matmul(psum[:, bank, :],
                                            qop[0:MAX_ROW, b, g * HG + j, qb * QB + t * P:qb * QB + (t + 1) * P],
                                            kop[0:MAX_ROW, b, g * HG + j, c * NH:(c + 1) * NH], start=True, stop=True)
                elif kind == "max_r":
                    last = rows_of_max(blk, c, bank)
                elif kind == "max_t":
                    pe.wait_ge(S["max_split"], blk + 1)
                    pe.wait_ge(S["in_c"], 32)
                    dst = psum[0:3 * HG * QT, bank, 0:P // 2].bitcast(BF16)
                    last = nc.tensor.transpose(dst, max_part[:, blk % 2, :, :], ident_bf)
                elif kind == "attn_t":
                    pe.wait_ge(S["slot_free"], r)
                    for q, tile in enumerate(range(*PIECES[blk])):
                        last = nc.tensor.transpose(psum[:, bank, q * P:(q + 1) * P], attn[:, tile, :, :], ident)
                else:
                    pe.wait_ge(S["o_copied"], blk + 1)
                    pe.wait_ge(S["in_ident"], 16)
                    for q in range(QT):
                        last = nc.tensor.transpose(psum[:, bank, q * P:(q + 1) * P],
                                                   o_sb[:, blk % 2, q * P:(q + 1) * P], ident)
                last.then_inc(S["slot_full"], 1)

            def scores(u, pair):
                blk, mt = divmod(u, TT)
                b, g, qb = BLOCKS[blk]
                s = PAIRS * u + pair
                if mt == 0 and pair == 0:
                    if blk == 0:
                        pe.wait_ge(S["rows0_in"], PAIRS)
                    elif blk < DIRECT:
                        pe.wait_ge(S["slot_free"], jobs_until("max_r", blk))
                    else:
                        pe.wait_ge(mrow_in[blk % 2], 16 * ((blk - DIRECT) // 2 + 1))
                if s >= len(ST_BANKS):
                    pe.wait_ge(S["exp_done"], s - len(ST_BANKS) + 1)
                elif s == 0:
                    pe.wait_ge(S["in_c"], 32)
                    pe.wait_ge(S["parts1_in"], HALVES)
                for i in range(2):
                    h = g * HG + 2 * pair + i
                    last = nc.tensor.matmul(psum[:, ST_BANKS[s % len(ST_BANKS)], i * QB:(i + 1) * QB],
                                            kop[0:SCORE_ROWS, b, h, mt * P:(mt + 1) * P],
                                            qop[0:SCORE_ROWS, b, h, qb * QB:(qb + 1) * QB],
                                            start=True, stop=True, skip_group_check=True)
                last.then_inc(S["st_full"], 1)

            def values(u):
                blk, mt = divmod(u, TT)
                b, g, qb = BLOCKS[blk]
                pe.wait_ge(S["exp_done"], PAIRS * (u + 1))
                if mt == 0 and blk:
                    pe.wait_ge(S["o_copied"], blk)
                if u == 0:
                    pe.wait_ge(S["v_ready"], 1)
                for j in range(HG):
                    last = nc.tensor.matmul(psum[j * VW:(j + 1) * VW, PV_BANK, 0:QB], v_aug[:, mt, b, g * HG + j, :],
                                            probs[:, u % P_RING, j, :], start=mt == 0, stop=mt == TT - 1,
                                            skip_group_check=True)
                last.then_inc(S["pv_done"], 1)

            def keep_warm(n, bank):
                for _ in range(n):
                    nc.tensor.matmul(psum[:, bank, 0:WARM_COLS], ident_bf, cbf_sb[:, 1:1 + WARM_COLS // P, :],
                                     start=True, stop=True, skip_group_check=True)

            def project(i):
                first, end = PIECES[i]
                pe.wait_ge(S["slot_free"], jobs_until("attn_t", i))
                if i == 0:
                    pe.wait_ge(S["in_rest"], 16 * IN_REST)
                nc.tensor.matmul(psum[:, PROJ_BANKS[first // 4], first % 4 * P:(first % 4 + end - first) * P], wo_sb[:],
                                 attn_t[:, first * P:end * P], start=True, stop=True,
                                 skip_group_check=True).then_inc(S["proj_full"], 1)

            for u in range(-LEAD, UNITS + 8):
                jobs = list(jobs_at[u])
                if u == EARLY + 2:
                    project(0)
                if u == UNITS - TT + PV_LAG + 4:
                    project(1)
                v = u - PV_LAG
                if 0 <= u < UNITS:
                    scores(u, 0)
                if 0 < v - 1 < UNITS and (v - 1) % TT == 0:
                    values(v - 1)

                for job in jobs[:HALVES]:
                    fill_slot(job)
                if 0 <= u < UNITS:
                    scores(u, 1)
                for job in jobs[HALVES:]:
                    fill_slot(job)
                if u + LEAD == TT + 1:
                    for c in range(PAIRS):
                        rows_of_max(0, c, ST_BANKS[c]).then_inc(S["rows0_full"], 1)
                if 0 <= v < UNITS and (v == 0 or v % TT):
                    values(v)

            keep_warm(6, PV_BANK)
            project(2)
            nc.tensor.matmul(psum[:, 6, 0:B * E], centre, rw_sb[:], start=True, stop=True).then_inc(S["crw_full"], 1)
            keep_warm(10, PV_BANK)
            pe.wait_ge(S["mean_ready"], 1)
            nc.tensor.matmul(psum[:, 4, 0:1], neg_avg, mean_b[:], start=True, stop=True).then_inc(S["mean_full"], 1)
            keep_warm(7, PV_BANK)
            pe.wait_ge(S["dev_ready"], 1)
            nc.tensor.matmul(psum[:, 5, 0:1], avg, dev[:], start=True, stop=True).then_inc(S["var_full"], 1)
            keep_warm(22, PV_BANK)
            for n, i in enumerate(LN1_ORDER):
                pe.wait_ge(S["t1_ready"], n + 1)
                for t in range(QUARTER):
                    last = nc.tensor.matmul(psum[:, CEN_BANKS[i], t * P:(t + 1) * P],
                                            t1[:, (QUARTER * i + t) * P:(QUARTER * i + t + 1) * P], centre,
                                            start=True, stop=True, skip_group_check=True)
                last.then_inc(S["cen1_full"], 1)
            keep_warm(22, PV_BANK)
            for t in range(TT):
                pe.wait_ge(S["z_ready"], t // QUARTER + 1)
                last = nc.tensor.matmul(psum[:, 6, 0:P], z[:, t, :], z[:, t, :], start=t == 0, stop=t == TT - 1)
            last.then_inc(S["gram0_full"], 1)
            for c in range(2):
                for t in range(4 * c, 4 * c + 4):
                    last = nc.tensor.transpose(psum[:, PROJ_BANKS[c], (t % 4) * P:(t % 4 + 1) * P], z[:, t, :], ident)
                last.then_inc(S["zt_full"], 1)
            for l in range(LAYERS):
                pe.wait_ge(S["gram_ready"], l + 1)
                if l:
                    pe.wait_ge(S["tt_ready"], l)
                for b in range(B):
                    for odd in range(2):
                        last = nc.tensor.matmul(psum[odd * C:(odd + 1) * C, (7, 5)[b], 0:NHEAD // 2 * C],
                                                gram[:, b * C:(b + 1) * C], vt_sb[:, l, odd, :],
                                                start=True, stop=True, skip_group_check=True)
                    last.then_inc(S["gv_full"], 1)
                nc.tensor.matmul(psum[:, 4, 0:C], ident_n, eye2_sb[:], start=True, stop=False, skip_group_check=True)
                for b in range(B):
                    pe.wait_ge(S[("gv_act", "gv_dve")[b]], l + 1)
                    for k in range(NHEAD // 2):
                        last = nc.tensor.matmul(psum[b * C:(b + 1) * C, 4, 0:C], q_pair[:, l, k, :], gv[:, b, k, :],
                                                start=False, stop=k == NHEAD // 2 - 1, skip_group_check=True)
                last.then_inc(S["m_full"], 1)
                pe.wait_ge(S["w_ready"], l + 1)
                if l < LAYERS - 1:
                    nc.tensor.matmul(psum[:, 6, 0:P], gram[:], w_l[:], start=True, stop=True).then_inc(S["u_full"], 1)
                    nc.tensor.matmul(psum[:, 7, 0:P], w_l[:], tt_l[:] if l else ident,
                                     start=True, stop=True).then_inc(S["tt_full"], 1)
                    pe.wait_ge(S["u_ready"], l + 1)
                    nc.tensor.matmul(psum[:, 5, 0:P], w_l[:], u_l[:], start=True, stop=True).then_inc(S["gram_full"], 1)
                else:
                    nc.tensor.matmul(psum[:, 7, 0:P], tt_l[:], w_l[:], start=True, stop=True).then_inc(S["tt_full"], 1)
            pe.wait_ge(S["tt_ready"], LAYERS)
            pe.wait_ge(S["zt_ready"], 2)
            for c in range(2):
                nc.tensor.matmul(psum[:, c, :], tt_f[:], z_t[:, c * NH:(c + 1) * NH],
                                 start=True, stop=True).then_inc(S["attn2_full"], 1)
            pe.wait_ge(S["crw_ready"], 1)
            for i in range(4):
                pe.wait_ge(S["t2_ready"], i // 2 + 1 if i < 3 else 3)
                for t in range(QUARTER * i, QUARTER * (i + 1)):
                    last = nc.tensor.matmul(cen2[:, t, 0:P + B * E], t2[:, t * P:(t + 1) * P], cen_rw[:],
                                            start=True, stop=True, skip_group_check=True)
                last.then_inc(S["cen2_full"], 1)
            keep_warm(44, YT_BANKS[3])
            for c in range(2):
                if c:
                    keep_warm(10, YT_BANKS[3])
                pe.wait_ge(S["y_ready"], TT * B // 2 * (c + 1))
                for b in range(B):
                    for t in range(4 * c, 4 * c + 4):
                        last = nc.tensor.transpose(psum[:, YT_BANKS[2 * c + b], (t % 4) * P:(t % 4 + 1) * P],
                                                   y[:, t, b, :, :], ident)
                    last.then_inc(S["yt_full"], 1)
            keep_warm(3, GB_BANKS[0])
            pe.wait_ge(S["logits_read"], 1)
            for c in range(2):
                pe.wait_ge(S["gate_split"], c + 1)
                for t in range(TT // 2):
                    last = nc.tensor.transpose(psum[:, GT_BANKS[c], t * P // 2:(t + 1) * P // 2].bitcast(BF16),
                                               gate_part[:, c * TT // 2 + t, :], ident_bf)
                last.then_inc(S["gt_full"], 1)
            pe.wait_ge(S["gt0_ready"], 1)
            pe.wait_ge(S["expb_split"], 1)
            for i in range(len(MOE) + GB_LAG):
                if i < len(MOE):
                    c, b, k = MOE[i]
                    if i < len(GB_BANKS) and GB_BANKS[i] in YT_BANKS:
                        pe.wait_ge(S["yt_ready"], YT_BANKS.index(GB_BANKS[i]) + 1)
                    if i < len(GB_BANKS) and GB_BANKS[i] in GT_BANKS:
                        pe.wait_ge(S["gt1_ready"], 1)
                    r = i - len(GB_BANKS)
                    if r in BY_DVE:
                        pe.wait_ge(S["scaled_dve"], BY_DVE.index(r) + 1)
                    elif r >= 0:
                        pe.wait_ge(S["gb_copied"], BY_POOL.index(r) + 1)
                    nc.tensor.matmul(psum[:, GB_BANKS[i % len(GB_BANKS)], :], select[:, b * (E // 2) + k, :],
                                     gate_t[:, c * NH:(c + 1) * NH], start=True, stop=True).then_inc(S["gb_full"], 1)
                r = i - GB_LAG
                if r >= 0:
                    c, b, k = MOE[r]
                    if b == 0 and k == 0:
                        for s in range(3):
                            nc.tensor.matmul(psum[:, MOE_BANKS[c], :], expb_part[:, s, :],
                                             gate_t[:, c * NH:(c + 1) * NH], start=s == 0, stop=False,
                                             skip_group_check=True)
                    if r in BY_DVE:
                        pe.wait_ge(S["scaled_dve"], BY_DVE.index(r) + 1)
                    else:
                        pe.wait_ge(S["scaled_pool"], BY_POOL.index(r) + 1)
                    nc.tensor.matmul(psum[b * C:(b + 1) * C, MOE_BANKS[c], :], expw_sb[:, k, :],
                                     scaled[:, r % SCALED, :], start=False, stop=k == E // 2 - 1,
                                     skip_group_check=True).then_inc(S["moe_done"], 1)

        @block.gpsimd
        def _(pool):
            def zero(op, b):
                return nc.gpsimd.memset(op[ZERO_FROM:MAX_ROW, b, :, :].bitcast(U32), 0)

            zero(kop, 0).then_inc(S["zeroed_k"], 1)
            pool.wait_ge(S["zeroed_k"], 1)
            nc.gpsimd.memset(v_aug[:], 0.0).then_inc(S["pool_chain"], 1)
            pool.wait_ge(S["pool_chain"], 1)
            nc.gpsimd.memset(v_aug[:, :, :, :, DH:DH + 1], 1.0).then_inc(S["zeroed_v"], 1)
            pool.wait_ge(S["zeroed_v"], 1)
            pool.wait_ge(S["v_out"], 2)
            pool.wait_ge(S["in_bv"], 16)
            v_at = v_aug[:, :, :, :, 0:DH].rearrange("p t b h d -> p t (b h) d")
            nc.gpsimd.tensor_tensor(v_at, v_at,
                                    bv_sb[:].rearrange("p (o h d) -> p o h d", o=1, d=DH).broadcast_to([P, TT, B * H, DH]),
                                    ALU.add).then_inc(S["v_ready"], 1)
            pool.wait_ge(S["v_ready"], 1)
            zero(kop, 1).then_inc(S["zeroed_k"], 1)
            pool.wait_ge(S["zeroed_k"], 2)
            zero(qop, 1).then_inc(S["zeroed_q1"], 1)
            pool.wait_ge(S["zeroed_q1"], 1)
            chain = [1]

            def link(ins):
                chain[0] += 1
                ins.then_inc(S["pool_chain"], 1)
                pool.wait_ge(S["pool_chain"], chain[0])

            split_done = {}

            def split(first, parts, rest_, last_inc):
                link(nc.gpsimd.tensor_copy(parts[0], first))
                link(nc.gpsimd.tensor_tensor(rest_, first, parts[0], ALU.subtract))
                link(nc.gpsimd.tensor_copy(parts[1], rest_))
                nc.gpsimd.tensor_tensor(parts[2], rest_, parts[1], ALU.subtract).then_inc(S[last_inc], 1)
                split_done[last_inc] = split_done.get(last_inc, 0) + 1
                pool.wait_ge(S[last_inc], split_done[last_inc])

            for blk in range(len(BLOCKS)):
                pool.wait_ge(S["max_ready"], blk + 1)
                if blk >= 2:
                    if blk == 2:
                        pool.wait_ge(S["rows0_full"], PAIRS)
                    else:
                        pool.wait_ge(S["slot_free"], jobs_until("max_r" if blk - 2 < DIRECT else "max_t", blk - 2))
                i = blk % 2
                split(negmax[:, i, :], [max_part[:, i, s, :] for s in range(3)], max_rest[:, i, :], "max_split")
                if blk == 0:
                    nc.gpsimd.memset(gate_part[:].bitcast(U32), 0).then_inc(S["gate_zeroed"], 1)
                    pool.wait_ge(S["gate_zeroed"], 1)
                if blk < HALVES:
                    at = slice(blk * NH, (blk + 1) * NH)
                    pool.wait_ge(S["parts1_in"], blk + 1)
                    split(rest[:, 1, at], [part[s][:, 1, at] for s in range(3)], rest[:, 1, at], "parts1")
                if blk == 10:
                    pool.wait_ge(S["in_rest"], 16 * IN_REST)
                    split(expb_sb[:], [expb_part[:, s, :] for s in range(3)], expb_rest[:], "expb_split")

            for n, i in enumerate(BY_POOL):
                c, b, k = MOE[i]
                pool.wait_ge(S["gb_copied"], n + 1)
                if i >= SCALED:
                    pool.wait_ge(S["moe_done"], i - SCALED + 1)
                if n == 0:
                    pool.wait_ge(S["yt_ready"], 4)
                nc.gpsimd.tensor_tensor(scaled[:, i % SCALED, :], gate_copy[:, n % 2, :],
                                        yt2[:, b, c * NH:(c + 1) * NH], ALU.mult).then_inc(S["scaled_pool"], 1)
                pool.wait_ge(S["scaled_pool"], n + 1)

        @block.scalar
        def _(act):
            act.wait_ge(S["warm"], 1)
            nc.scalar.activation(warm[:, 1:2], warm[:, 0:1], ACT.Exp).then_inc(S["warm"], 1)
            act.wait_ge(S["in_qk"], 32)
            for hf in range(HALVES):
                act.wait_ge(S["qk_full"], hf + 1)
                nc.scalar.activation(part[0][:, 0, hf * NH:(hf + 1) * NH], psum[:, 4 + hf, :],
                                     ACT.Identity, bias=cols_sb[:, 0:1]).then_inc(S["part_h"], 1)
            for hf in range(HALVES):
                act.wait_ge(S["part_r"], hf + 1)
                nc.scalar.activation(part[1][:, 0, hf * NH:(hf + 1) * NH], rest[:, 0, hf * NH:(hf + 1) * NH],
                                     ACT.Copy).then_inc(S["part_m"], 1)
            act.wait_ge(S["zeroed_v"], 1)
            for hf in range(2):
                act.wait_ge(S["v_full"], hf + 1)
                nc.scalar.activation(v_aug[:, 4 * hf:4 * hf + 4, :, :, 0:DH].rearrange("p t b h d -> p t (b h) d"),
                                     psum[:, 2 + hf, :].rearrange("p (t h d) -> p t h d", t=4, d=DH),
                                     ACT.Copy).then_inc(S["v_out"], 1)
            act.wait_ge(S["zeroed_k"], 1)
            act.wait_ge(S["zeroed_q"], 1)
            for i in range(len(SELECTED)):
                if i == 1:
                    continue
                what, a, hf = SELECTED[i]
                act.wait_ge(S["sel_full"], i + 1)
                bank = psum[0:MAX_ROW, SEL_BANKS[i], :]
                if what == "q":
                    nc.scalar.activation(qop[0:MAX_ROW, 0, 2 * a:2 * a + 2, 0:QB],
                                         bank.rearrange("p (h n) -> p h n", h=2), ACT.Copy).then_inc(S["sel_act"], 1)
                else:
                    nc.scalar.activation(kop[0:MAX_ROW, 0, a, hf * NH:(hf + 1) * NH], bank, ACT.Copy).then_inc(S["sel_act"], 1)
            for hf in range(HALVES):
                act.wait_ge(S["qk_full"], HALVES + hf + 1)
                nc.scalar.activation(rest[:, 1, hf * NH:(hf + 1) * NH], psum[:, 6 + hf, :],
                                     ACT.Identity, bias=cols_sb[:, 0:1]).then_inc(S["parts1_in"], 1)
            for c in range(PAIRS):
                act.wait_ge(S["rows0_full"], c + 1)
                nc.scalar.activation(qop[MAX_ROW:SCORE_ROWS, 0, c * PAIRS:(c + 1) * PAIRS, 0:QB],
                                     psum[MAX_ROW:SCORE_ROWS, ST_BANKS[c], :].rearrange("p (h n) -> p h n", h=PAIRS),
                                     ACT.Copy).then_inc(S["rows0_in"], 1)
            for u in range(UNITS + PV_LAG + 1):
                if u < UNITS:
                    if u >= P_RING:
                        act.wait_ge(S["pv_done"], u - P_RING + 1)
                    for pair in range(PAIRS):
                        s = PAIRS * u + pair
                        act.wait_ge(S["st_full"], s + 1)
                        nc.scalar.activation(probs[:, u % P_RING, 2 * pair:2 * pair + 2, :],
                                             psum[:, ST_BANKS[s % len(ST_BANKS)], :].rearrange("p (i n) -> p i n", i=2),
                                             ACT.Exp, scale=SCALE).then_inc(S["exp_done"], 1)
                w = u - PV_LAG - (TT - 1)
                if w >= 0 and w % TT == 0:
                    blk = w // TT
                    act.wait_ge(S["pv_done"], TT * (blk + 1))
                    if blk >= 2:
                        act.wait_ge(S["slot_free"], jobs_until("out_t", blk - 2))
                    nc.scalar.activation(o_sb[:, blk % 2, :], psum[:, PV_BANK, 0:QB], ACT.Copy).then_inc(S["o_copied"], 1)

            nc.scalar.activation(warm[:, 1:2], warm[:, 0:1], ACT.Sqrt).then_inc(S["warm"], 1)
            act.wait_ge(S["crw_full"], 1)
            nc.scalar.activation(cen_rw[:, P:], psum[:, 6, 0:B * E], ACT.Copy).then_inc(S["crw_ready"], 1)

            def roots(i, n):
                act.wait_ge(S["var_ready"], i + 1)
                nc.scalar.activation(root[:, 0:n], var_eps[:, 0:n], ACT.Sqrt).then_inc(S["root_ready"], 1)

            roots(0, 1)
            act.wait_ge(S["aff_ready"], 1)
            nc.scalar.activation(aff[:, 0:NH], psum[:, PROJ_BANKS[0], :], ACT.Identity,
                                 bias=shift[:], scale=gain[:]).then_inc(S["affine_done"], 1)
            for n, i in enumerate(LN1_ORDER):
                act.wait_ge(S["cen1_full"], n + 1)
                nc.scalar.activation(sq[:, QUARTER * i:QUARTER * (i + 1), :],
                                     psum[:, CEN_BANKS[i], 0:QUARTER * P].rearrange("p (t c) -> p t c", c=P),
                                     ACT.Square).then_inc(S["sq1_ready"], 1)
            roots(1, TT * B)
            for c in range(2):
                act.wait_ge(S["zt_full"], c + 1)
                nc.scalar.activation(z_t[:, c * NH:(c + 1) * NH], psum[:, PROJ_BANKS[c], :], ACT.Copy).then_inc(S["zt_ready"], 1)
            for l in range(LAYERS):
                act.wait_ge(S["gv_full"], 2 * l + 1)
                nc.scalar.activation(gv[:, 0, :, :],
                                     psum[:, 7, 0:NHEAD * C // 2].rearrange("p (j c) -> p j c", c=C),
                                     ACT.Copy).then_inc(S["gv_act"], 1)
                act.wait_ge(S["tt_full"], l + 1)
                nc.scalar.activation(tt_l[:] if l < LAYERS - 1 else tt_f[:], psum[:, 7, 0:P],
                                     ACT.Copy).then_inc(S["tt_ready"], 1)
            for i in range(4):
                act.wait_ge(S["cen2_full"], i + 1)
                at = slice(QUARTER * i, QUARTER * (i + 1))
                nc.scalar.activation(sq[:, at, :], cen2[:, at, 0:P], ACT.Square).then_inc(S["sq2_ready"], 1)
            roots(2, TT * B)

            nc.scalar.activation(warm[:, 1:2], warm[:, 0:1], ACT.Exp).then_inc(S["warm"], 1)
            act.wait_ge(S["logits_read"], 1)
            for t in range(TT):
                if t == TT - 2:
                    act.wait_ge(S["delta_ready"], 1)
                    nc.scalar.activation(ed[:], dlt[:], ACT.Exp).then_inc(S["exp2_ready"], 1)
                for b in range(B):
                    nc.scalar.activation(y[:, t, b, :, :],
                                         cen2[:, t:t + 1, b * C:(b + 1) * C].broadcast_to([P, 2, C]), ACT.Copy,
                                         scale=rstd[:, t * B + b:t * B + b + 1]).then_inc(S["y_ready"], 1)
            for i in range(4):
                c, b = divmod(i, 2)
                act.wait_ge(S["yt_full"], i + 1)
                nc.scalar.activation(yt2[:, b, c * NH:(c + 1) * NH], psum[:, YT_BANKS[i], :],
                                     ACT.Copy).then_inc(S["yt_ready"], 1)
            act.wait_ge(S["gt_full"], 2)
            nc.scalar.activation(gate_t[:, NH:], psum[:, GT_BANKS[1], 0:NH // 2].bitcast(BF16),
                                 ACT.Copy).then_inc(S["gt1_ready"], 1)
            for n, i in enumerate(BY_POOL):
                act.wait_ge(S["gb_full"], i + 1)
                if n >= 2:
                    act.wait_ge(S["scaled_pool"], n - 1)
                nc.scalar.activation(gate_copy[:, n % 2, :], psum[:, GB_BANKS[i % len(GB_BANKS)], :],
                                     ACT.Copy).then_inc(S["gb_copied"], 1)

        @block.vector
        def _(dve):
            V = nc.vector
            chain = [0]

            def link(ins):
                chain[0] += 1
                ins.then_inc(S["dve_chain"], 1)
                dve.wait_ge(S["dve_chain"], chain[0])

            V.memset(idle[:].bitcast(U32), 0).then_inc(S["idle_ready"], 1)
            V.memset(warm[:], 0.0).then_inc(S["warm"], 1)
            V.memset(qop[ZERO_FROM:MAX_ROW, 0, :, :].bitcast(U32), 0).then_inc(S["zeroed_q"], 1)
            for hf in range(HALVES):
                at = slice(hf * NH, (hf + 1) * NH)
                dve.wait_ge(S["part_h"], hf + 1)
                V.scalar_tensor_tensor(out=rest[:, 0, at], in0=psum[:, 4 + hf, :],
                                       scalar=cols_sb[:, 0:1], in1=part[0][:, 0, at], op0=ALU.add,
                                       op1=ALU.subtract).then_inc(S["part_r"], 1)
            for hf in range(HALVES):
                at = slice(hf * NH, (hf + 1) * NH)
                dve.wait_ge(S["part_m"], hf + 1)
                V.tensor_tensor(part[2][:, 0, at], rest[:, 0, at], part[1][:, 0, at],
                                ALU.subtract).then_inc(S["part_l"], 1)
            dve.wait_ge(S["zeroed_k"], 1)
            dve.wait_ge(S["sel_full"], 2)
            V.tensor_copy(kop[0:MAX_ROW, 0, 0, 0:NH], psum[0:MAX_ROW, SEL_BANKS[1], :]).then_inc(S["sel_dve"], 1)

            for r, (kind, blk, k, c) in enumerate(SLOT_JOBS):
                bank = slot_bank[r]
                b, g, qb = BLOCKS[blk]
                i = blk % 2
                dve.wait_ge(S["slot_full"], r + 1)
                if kind == "max":
                    if k == 0 and c == 0 and blk >= 2:
                        dve.wait_ge(S["max_split"], blk - 1)
                    V.tensor_reduce(negmax_half[:, i, c, k:k + 1], psum[:, bank, :], AX_X, ALU.max,
                                    negate=True).then_inc(S["slot_free"], 1)
                    if k == TT - 1 and c == HALVES - 1:
                        dve.wait_ge(S["slot_free"], r + 1)
                        V.tensor_tensor(negmax[:, i, :], negmax_half[:, i, 0, :], negmax_half[:, i, 1, :],
                                        ALU.min).then_inc(S["max_ready"], 1)
                elif kind == "max_r":
                    h = g * HG + c * PAIRS
                    V.tensor_copy(qop[MAX_ROW:SCORE_ROWS, b, h:h + PAIRS, qb * QB:(qb + 1) * QB],
                                  psum[MAX_ROW:SCORE_ROWS, bank, :].rearrange("p (h n) -> p h n", h=PAIRS)
                                  ).then_inc(S["slot_free"], 1)
                elif kind == "max_t":
                    if blk >= DIRECT + 2:
                        dve.wait_ge(mrow_in[i], 16 * ((blk - DIRECT) // 2))
                    V.tensor_copy(max_row[:, i, :], psum[0:3 * HG * QT, bank, 0:P // 2].bitcast(BF16)
                                  ).then_inc(S["slot_free"], 1)
                elif kind == "attn_t":
                    first, end = PIECES[blk]
                    V.tensor_copy(attn_t[:, first * P:end * P], psum[:, bank, 0:(end - first) * P]).then_inc(S["slot_free"], 1)
                    dve.wait_ge(S["proj_full"], blk + 1)
                    for n in range(first // QT, end // QT):
                        at = n * QB % NH
                        last = V.bn_stats(bn[:, n, :], psum[:, PROJ_BANKS[n * QB // NH], at:at + QB])
                    link(last)
                else:
                    o = psum[:, bank, 0:QT * P].rearrange("p (t j v) -> p t j v", t=QT, j=HG)
                    link(V.reciprocal(rden[:, i, :, :], o[:, :, :, DH]))
                    dst = attn[:, qb * QT:(qb + 1) * QT, b, g * HG * DH:(g + 1) * HG * DH]
                    V.tensor_tensor(dst.rearrange("p t (j d) -> p t j d", j=HG), o[:, :, :, 0:DH],
                                    rden[:, i, :, :].rearrange("p t (j o) -> p t j o", o=1).broadcast_to([P, QT, HG, DH]),
                                    ALU.mult).then_inc(S["slot_free"], 1)

            link(V.bn_aggr(mv[:], bn[:].rearrange("p a b -> p (a b)")))
            V.tensor_tensor(mean_b[:], mv[:, 0:1], cols_sb[:, 1:2], ALU.add).then_inc(S["mean_ready"], 1)
            dve.wait_ge(S["mean_full"], 1)
            dve.wait_ge(S["mean_ready"], 1)
            link(V.tensor_tensor(diff[:], psum[:, 4, 0:1], mean_b[:], ALU.add))
            V.scalar_tensor_tensor(out=dev[:], in0=diff[:], scalar=diff[:], in1=mv[:, 1:2], op0=ALU.mult,
                                   op1=ALU.add).then_inc(S["dev_ready"], 1)
            link(V.tensor_tensor(neg_mean[:], psum[:, 4, 0:1], cols_sb[:, 1:2], ALU.add))

            def reciprocal_root(i, variance, scale, out, n):
                v, y0, w = var_eps[:, 0:n], root[:, 0:n], newton[:, 0:n]
                V.tensor_scalar(v, variance, scale, EPS, ALU.mult, ALU.add).then_inc(S["var_ready"], 1)
                dve.wait_ge(S["var_ready"], i + 1)
                dve.wait_ge(S["root_ready"], i + 1)
                link(V.reciprocal(y0, y0))
                link(V.tensor_tensor(w, y0, y0, ALU.mult))
                link(V.scalar_tensor_tensor(out=w, in0=w, scalar=-0.5, in1=v, op0=ALU.mult, op1=ALU.mult))
                return V.scalar_tensor_tensor(out=out, in0=w, scalar=1.5, in1=y0, op0=ALU.add, op1=ALU.mult)

            dve.wait_ge(S["var_full"], 1)
            link(reciprocal_root(0, psum[:, 5, 0:1], 1.0, grstd[:], 1))
            link(V.tensor_tensor(gain[:], grstd[:], cols_sb[:, 2:3], ALU.mult))
            V.scalar_tensor_tensor(out=shift[:], in0=neg_mean[:], scalar=gain[:], in1=cols_sb[:, 3:4], op0=ALU.mult,
                                   op1=ALU.add).then_inc(S["aff_ready"], 1)
            dve.wait_ge(S["aff_ready"], 1)
            def quarter(i):
                return slice(i * QB, (i + 1) * QB)

            link(V.tensor_scalar(aff[:, NH:], x_sb[:, NH:], shift[:], None, ALU.add))
            for i in LN1_ORDER:
                at = quarter(i)
                if i >= 2:
                    last = V.scalar_tensor_tensor(out=t1[:, at], in0=psum[:, PROJ_BANKS[1], quarter(i - 2)],
                                                  scalar=gain[:], in1=aff[:, at], op0=ALU.mult, op1=ALU.add)
                else:
                    dve.wait_ge(S["affine_done"], 1)
                    last = V.tensor_tensor(t1[:, at], aff[:, at], x_sb[:, at], ALU.add)
                last.then_inc(S["t1_ready"], 1)

            def token_rstd(norm):
                for n, i in enumerate(LN1_ORDER if norm == 1 else range(4)):
                    dve.wait_ge(S[f"sq{norm}_ready"], n + 1)
                    last = V.tensor_reduce(ssq[:, 4 * i:4 * i + 4],
                                           sq[:, QUARTER * i:QUARTER * (i + 1), :].rearrange("p t (b c) -> p (t b) c", b=B),
                                           AX_X, ALU.add)
                link(last)
                return reciprocal_root(norm, ssq[:], 1.0 / C, rstd[:], TT * B)

            link(token_rstd(1))
            for i in range(4):
                V.tensor_tensor(z[:, QUARTER * i:QUARTER * (i + 1), :].rearrange("p t (b c) -> p t b c", b=B),
                                psum[:, CEN_BANKS[i], 0:QUARTER * P].rearrange("p (t b c) -> p t b c", b=B, c=C),
                                rstd[:, 4 * i:4 * i + 4].rearrange("p (t b o) -> p t b o", b=B, o=1)
                                .broadcast_to([P, QUARTER, B, C]), ALU.mult).then_inc(S["z_ready"], 1)
            dve.wait_ge(S["gram0_full"], 1)
            V.tensor_tensor(gram[:], psum[:, 6, 0:P], diag_mask, ALU.mult).then_inc(S["gram_ready"], 1)
            for l in range(LAYERS):
                dve.wait_ge(S["gv_full"], 2 * l + 2)
                V.tensor_copy(gv[:, 1, :, :],
                              psum[:, 5, 0:NHEAD * C // 2].rearrange("p (j c) -> p j c", c=C)).then_inc(S["gv_dve"], 1)
                dve.wait_ge(S["m_full"], l + 1)
                V.scalar_tensor_tensor(out=w_l[:].rearrange("p (b c) -> p b c", b=B),
                                       in0=psum[:, 4:5, 0:C].broadcast_to([P, B, C]), scalar=1.0 / (N * NHEAD),
                                       in1=diag_mask.rearrange("p (b c) -> p b c", b=B),
                                       op0=ALU.mult, op1=ALU.mult).then_inc(S["w_ready"], 1)
                if l < LAYERS - 1:
                    dve.wait_ge(S["u_full"], l + 1)
                    V.tensor_copy(u_l[:], psum[:, 6, 0:P]).then_inc(S["u_ready"], 1)
                    dve.wait_ge(S["gram_full"], l + 1)
                    V.tensor_copy(gram[:], psum[:, 5, 0:P]).then_inc(S["gram_ready"], 1)
            for first, size in ((0, NH), (NH, QB), (NH + QB, QB)):
                dve.wait_ge(S["attn2_full"], first // NH + 1)
                V.tensor_tensor(t2[:, first:first + size], psum[:, first // NH, first % NH:first % NH + size],
                                t1[:, first:first + size], ALU.add).then_inc(S["t2_ready"], 1)
            token_rstd(2).then_inc(S["rstd_ready"], 1)
            dve.wait_ge(S["rstd_ready"], 1)

            G8 = TT * B // 2

            def halves(step):
                for c in range(2):
                    dve.wait_ge(S["dve_chain"], chain[0] - 1)
                    chain[0] += 1
                    step(c).then_inc(S["dve_chain"], 1)

            def of(v, c):
                return v[:, c * G8:(c + 1) * G8]

            def over_e(v, c):
                return of(v, c).rearrange("p (a o) -> p a o", o=1).broadcast_to([P, G8, E])

            def over_tokens(v):
                return v[:].rearrange("p (o e) -> p o e", o=1).broadcast_to([P, G8, E])

            dve.wait_ge(S["in_rest"], 16 * IN_REST)
            V.tensor_tensor(lg[:].rearrange("p (t b) e -> p t b e", b=B),
                            cen2[:, :, P:P + B * E].rearrange("p t (b e) -> p t b e", b=B),
                            rstd[:].rearrange("p (t b o) -> p t b o", b=B, o=1).broadcast_to([P, TT, B, E]),
                            ALU.mult).then_inc(S["logits_read"], 1)
            dve.wait_ge(S["logits_read"], 1)
            halves(lambda c: V.tensor_tensor(of(lg, c), of(lg, c), over_tokens(rb_sb), ALU.add))

            def one_hot_of_largest(logits, largest, hot):
                halves(lambda c: V.tensor_reduce(of(largest, c), of(logits, c), AX_X, ALU.max))
                halves(lambda c: V.tensor_tensor(of(cand, c), of(logits, c), over_e(largest, c), ALU.is_equal))
                halves(lambda c: V.tensor_tensor(of(cand, c), of(cand, c), over_tokens(weight_sb), ALU.mult))
                halves(lambda c: V.tensor_reduce(of(pick, c), of(cand, c), AX_X, ALU.max))
                halves(lambda c: V.tensor_tensor(of(hot, c), over_tokens(weight_sb), over_e(pick, c), ALU.is_equal))

            one_hot_of_largest(lg, m1, hot1)
            halves(lambda c: V.scalar_tensor_tensor(out=of(lg2, c), in0=of(hot1, c), scalar=-3e38, in1=of(lg, c),
                                                    op0=ALU.mult, op1=ALU.add))
            one_hot_of_largest(lg2, m2, hot2)
            V.tensor_tensor(dlt[:], m2[:], m1[:], ALU.subtract).then_inc(S["delta_ready"], 1)
            dve.wait_ge(S["exp2_ready"], 1)
            link(V.tensor_scalar(gate1[:], ed[:], 1.0, None, ALU.add))
            halves(lambda c: V.tensor_tensor(of(hot2, c), of(hot2, c), over_e(ed, c), ALU.mult))
            link(V.reciprocal(gate1[:], gate1[:]))
            halves(lambda c: V.tensor_tensor(of(gates, c), of(hot1, c), of(hot2, c), ALU.add))
            halves(lambda c: V.tensor_tensor(of(gates, c), of(gates, c), over_e(gate1, c), ALU.mult))
            dve.wait_ge(S["gate_zeroed"], 1)

            def by_tile(v, c):
                return of(v, c).rearrange("p (t b) e -> p t (b e)", b=B)

            def gp(s, c):
                return gate_part[:, c * TT // 2:(c + 1) * TT // 2, s * B * E:(s + 1) * B * E]

            halves(lambda c: V.tensor_copy(gp(0, c), by_tile(gates, c)))
            halves(lambda c: V.tensor_tensor(by_tile(gate_rest, c), by_tile(gates, c), gp(0, c), ALU.subtract))
            halves(lambda c: V.tensor_copy(gp(1, c), by_tile(gate_rest, c)))
            for c in range(2):
                dve.wait_ge(S["dve_chain"], chain[0] - 1 + c)
                V.tensor_tensor(gp(2, c), by_tile(gate_rest, c), gp(1, c), ALU.subtract).then_inc(S["gate_split"], 1)
            dve.wait_ge(S["gt_full"], 1)
            V.tensor_copy(gate_t[:, 0:NH], psum[:, GT_BANKS[0], 0:NH // 2].bitcast(BF16)).then_inc(S["gt0_ready"], 1)
            for n, i in enumerate(BY_DVE):
                c, b, k = MOE[i]
                dve.wait_ge(S["gb_full"], i + 1)
                dve.wait_ge(S["yt_ready"], 2 * c + b + 1)
                if i >= SCALED:
                    dve.wait_ge(S["moe_done"], i - SCALED + 1)
                V.tensor_tensor(scaled[:, i % SCALED, :], psum[:, GB_BANKS[i % len(GB_BANKS)], :],
                                yt2[:, b, c * NH:(c + 1) * NH], ALU.mult).then_inc(S["scaled_dve"], 1)
                if i == BY_DVE[-3]:
                    dve.wait_ge(S["moe_done"], len(MOE) // 2)
                    V.tensor_tensor(res[:, 0:NH], psum[:, MOE_BANKS[0], :], t2[:, 0:NH], ALU.add).then_inc(S["out_done"], 1)
            dve.wait_ge(S["moe_done"], len(MOE))
            for first, end in OUT_PIECES[1:]:
                V.tensor_tensor(res[:, first:end], psum[:, MOE_BANKS[1], first - NH:end - NH], t2[:, first:end],
                                ALU.add).then_inc(S["out_done"], 1)


def kernel(**inputs):
    import numpy as np
    import concourse.bacc as bacc
    from concourse.bass_utils import run_bass_kernel_spmd

    f32 = np.float32
    get = {k.removeprefix("L0_conv_").removeprefix("L1_"): np.asarray(v, f32) for k, v in inputs.items()}

    def diag(a, n=B):
        out = np.zeros((n * a.shape[0], n * a.shape[1]), a.dtype)
        for i in range(n):
            out[i * a.shape[0]:(i + 1) * a.shape[0], i * a.shape[1]:(i + 1) * a.shape[1]] = a
        return out

    x = get["x"].reshape(P, N)

    def by_channel(q, k):
        return np.stack([q, k]).reshape(2, H, DH, -1).transpose(2, 0, 1, 3).reshape(P, -1)

    qk = by_channel(get["Wq"], get["Wk"]).T
    wqk = np.zeros((P, B, P), f32)
    for b in range(B):
        wqk[b * C:(b + 1) * C, b] = qk
    cols = np.stack([by_channel(get["bq"], get["bk"])[:, 0]] + [np.tile(get[n], B) for n in ("bo", "gn_w", "gn_b")], 1)
    bv_row = np.broadcast_to(np.tile(get["bv"], B), (P, P))
    v, q = get["attn_v_matrix"][:, :, 0], get["attn_q_matrix"][:, :, 0]
    by_parity = v.reshape(LAYERS, NHEAD // 2, 2, C, C)
    vt = np.tile(by_parity.transpose(4, 0, 2, 1, 3).reshape(C, LAYERS, 2, NHEAD // 2 * C), (B, 1, 1, 1))
    q_pairs = q.reshape(LAYERS, NHEAD // 2, 2, C, C).transpose(2, 4, 0, 1, 3).reshape(P, LAYERS, NHEAD // 2, C)
    cen_r = diag(get["ffn_router_w"])
    expw = get["ffn_expert_w"].reshape(E // 2, 2 * C, C).transpose(1, 0, 2)
    expb = np.zeros((P, P), f32)
    expb[:3 * B * E] = np.tile(diag(get["ffn_expert_b"]), (3, 1))
    rb_row = np.broadcast_to(get["ffn_router_b"], (P, E))

    eye = np.eye(P, dtype=f32)
    group = C // 8
    avg = np.kron(np.eye(P // group), np.full((group, group), 1.0 / group)).astype(f32)
    centre = eye - diag(np.full((C, C), 1.0 / C, f32))
    consts = np.concatenate([eye, centre, -avg, avg, diag(np.ones((C, C), f32)), eye * (N * NHEAD),
                             np.broadcast_to(np.arange(E, 0, -1, dtype=f32), (P, E)), np.tile(np.eye(C, dtype=f32), (B, 1))], 1)
    select = np.zeros((P, B * E // 2, P), f32)
    for s in range(3):
        for b in range(B):
            for e in range(E):
                select[(s * B + b) * E + e, b * (E // 2) + e // 2, (e % 2) * C:(e % 2 + 1) * C] = 1
    take = np.zeros((P, 2, HG, PARTS, MAX_ROW), f32)
    for w in range(2):
        for h in range(HG):
            for r in range(PARTS):
                for s in range(PARTS):
                    for d in range(DH):
                        take[(d * 2 + w) * H + h, w, h, (r * w + s) % PARTS, (r * PARTS + s) * DH + d] = 1
    import ml_dtypes
    bf = ml_dtypes.bfloat16
    cbf = np.concatenate([eye.astype(bf), select.reshape(P, -1).astype(bf)], 1)
    ones = np.ones((3, B, H, N), bf)

    nc = bacc.Bacc("TRN2", target_bir_lowering=False, num_devices=1)
    arrays, args = {}, []
    for name, a in dict(x=x, wqk=wqk, sel=take.astype(bf), wv=diag(get["Wv"].T.copy()), wo=diag(get["Wo"].T.copy()), cols=cols, bv_row=bv_row, vt=vt,
                        q_pairs=q_pairs, router=cen_r, expw=expw, expb=expb, rb_row=rb_row, consts=consts, cbf=cbf,
                        ones=ones).items():
        a = np.ascontiguousarray(a)
        arrays[f"in_{name}"] = a
        args.append(nc.dram_tensor(f"in_{name}", a.shape, mybir.dt.from_np(a.dtype), kind="ExternalInput").ap())
    args.append(nc.dram_tensor("out", (P, N), F32, kind="ExternalOutput").ap())
    conv_attn_hybrid_kernel(nc, *args)
    r = run_bass_kernel_spmd(nc, [arrays], core_ids=[0])
    return r.results[0]["out"].reshape(B, C, 32, 32)
```
